# Optimizing a Trainium2 kernel written in Bass

```python
import numpy as np
import jax
import jax.numpy as jnp

def _softmax(x, axis=-1):
    return jax.nn.softmax(x, axis=axis)

def _gelu(x):
    return jax.nn.gelu(x, approximate=True)

def _silu(x):
    return jax.nn.silu(x)

def _sigmoid(x):
    return jax.nn.sigmoid(x)

def _layernorm(x, axis=-1, eps=1e-05):
    m = jnp.mean(x, axis=axis, keepdims=True)
    v = jnp.var(x, axis=axis, keepdims=True)
    return (x - m) / jnp.sqrt(v + eps)

def _scatter_add(tgt, idx, src, axis=0):
    return tgt.at[idx].add(src)

def _segment_sum(src, seg, n):
    return jax.ops.segment_sum(src, seg, n)
kernel_name = 'mk_hybrid_d1_jaxref_r8_8fa225'

def setup_inputs(seed: int=0):
    np.random.seed(seed)
    _w = jnp.asarray

    def _L0_attn_a_setup():
        import jax, jax.numpy as jnp
        import numpy as np
        HID = 128
        NH = 16
        HD = HID // NH
        WIN = 64
        EPS = 1e-05

        def layernorm(x, g, b):
            m = jnp.mean(x, axis=-1, keepdims=True)
            v = jnp.mean((x - m) ** 2, axis=-1, keepdims=True)
            return (x - m) / jnp.sqrt(v + EPS) * g + b

        def windowed_attention(q, k, v, window_size):
            bh, S, D = q.shape
            scale = float(D) ** (-0.5)
            w2, w4 = (window_size // 2, window_size // 4)
            out = jnp.zeros_like(q)
            for i in range(0, S, w2):
                start = max(0, i - w4)
                end = min(S, i + window_size - w4)
                qw = q[:, start:end] * scale
                kw = k[:, start:end]
                vw = v[:, start:end]
                attn = jax.nn.softmax(jnp.einsum('bqd,bkd->bqk', qw, kw), axis=-1)
                wo = jnp.einsum('bqk,bkd->bqd', attn, vw)
                if i == 0:
                    out = out.at[:, start:end].set(wo)
                else:
                    oe = min(i + w4, S)
                    n = oe - start
                    alphas = jnp.linspace(0.0, 1.0, n).reshape(1, -1, 1)
                    blended = (1 - alphas) * out[:, start:oe] + alphas * wo[:, :n]
                    out = out.at[:, start:oe].set(blended)
                    out = out.at[:, oe:end].set(wo[:, n:end - start])
            return out
        key = jax.random.key(seed)
        ks = jax.random.split(key, 12)
        s = 0.02
        d = {'hidden_states': jax.random.normal(ks[0], (4, 256, HID), jnp.float32), 'ln1_g': jnp.ones((HID,), jnp.float32), 'ln1_b': jnp.zeros((HID,), jnp.float32), 'wq': jax.random.normal(ks[1], (HID, HID), jnp.float32) * s, 'bq': jnp.zeros((HID,), jnp.float32), 'wk': jax.random.normal(ks[2], (HID, HID), jnp.float32) * s, 'bk': jnp.zeros((HID,), jnp.float32), 'wv': jax.random.normal(ks[3], (HID, HID), jnp.float32) * s, 'bv': jnp.zeros((HID,), jnp.float32), 'wproj': jax.random.normal(ks[4], (HID, HID), jnp.float32) * s, 'bproj': jnp.zeros((HID,), jnp.float32), 'ln2_g': jnp.ones((HID,), jnp.float32), 'ln2_b': jnp.zeros((HID,), jnp.float32), 'w1': jax.random.normal(ks[5], (HID, 4 * HID), jnp.float32) * s, 'b1': jnp.zeros((4 * HID,), jnp.float32), 'w2': jax.random.normal(ks[6], (4 * HID, HID), jnp.float32) * s, 'b2': jnp.zeros((HID,), jnp.float32)}
        return d
    _L0_attn_a_in = _L0_attn_a_setup()

    def _L0_attn_b_setup():
        import jax, jax.numpy as jnp
        import numpy as np
        D_MODEL = 128
        N_HEADS = 16
        HEAD_DIM = D_MODEL // N_HEADS
        WINDOW = 128

        def _window_starts(seq_len, window):
            starts = []
            for i in range(0, seq_len, window // 2):
                end = min(i + window, seq_len)
                starts.append(max(0, end - window))
                if end == seq_len:
                    break
            return np.asarray(starts, dtype=np.int32)
        key = jax.random.key(seed)
        ks = jax.random.split(key, 9)
        B, S = (4, 512)
        sc = 1.0 / np.sqrt(D_MODEL)
        return {'x': jax.random.normal(ks[0], (B, S, D_MODEL), jnp.float32), 'Wq': jax.random.normal(ks[1], (D_MODEL, D_MODEL), jnp.float32) * sc, 'bq': jax.random.normal(ks[2], (D_MODEL,), jnp.float32) * 0.02, 'Wk': jax.random.normal(ks[3], (D_MODEL, D_MODEL), jnp.float32) * sc, 'bk': jax.random.normal(ks[4], (D_MODEL,), jnp.float32) * 0.02, 'Wv': jax.random.normal(ks[5], (D_MODEL, D_MODEL), jnp.float32) * sc, 'bv': jax.random.normal(ks[6], (D_MODEL,), jnp.float32) * 0.02, 'Wo': jax.random.normal(ks[7], (D_MODEL, D_MODEL), jnp.float32) * sc, 'bo': jax.random.normal(ks[8], (D_MODEL,), jnp.float32) * 0.02}
    _L0_attn_b_in = _L0_attn_b_setup()

    def _L0_ffn_setup():
        import jax, jax.numpy as jnp
        import numpy as np
        B, T, D = (2, 256, 128)
        E, DFF, TOPK = (8, 512, 2)
        TEMPERATURE = 1.0
        key = jax.random.key(seed)
        k_x, k_w1, k_w2, k_r = jax.random.split(key, 4)
        x = jax.random.normal(k_x, (B, T, D), dtype=jnp.float32)
        W1 = jax.random.normal(k_w1, (E, DFF, D), dtype=jnp.float32) * 0.02
        W2 = jax.random.normal(k_w2, (E, D, DFF), dtype=jnp.float32) * 0.02
        Wr = jax.random.normal(k_r, (E, D), dtype=jnp.float32) * 0.02
        return {'x': x, 'W1': W1, 'W2': W2, 'Wr': Wr}
    _L0_ffn_in = _L0_ffn_setup()
    _d = {'L0_attn_a_hidden_states': _L0_attn_a_in['hidden_states'], 'L0_attn_a_ln1_g': _L0_attn_a_in['ln1_g'], 'L0_attn_a_ln1_b': _L0_attn_a_in['ln1_b'], 'L0_attn_a_wq': _L0_attn_a_in['wq'], 'L0_attn_a_bq': _L0_attn_a_in['bq'], 'L0_attn_a_wk': _L0_attn_a_in['wk'], 'L0_attn_a_bk': _L0_attn_a_in['bk'], 'L0_attn_a_wv': _L0_attn_a_in['wv'], 'L0_attn_a_bv': _L0_attn_a_in['bv'], 'L0_attn_a_wproj': _L0_attn_a_in['wproj'], 'L0_attn_a_bproj': _L0_attn_a_in['bproj'], 'L0_attn_a_ln2_g': _L0_attn_a_in['ln2_g'], 'L0_attn_a_ln2_b': _L0_attn_a_in['ln2_b'], 'L0_attn_a_w1': _L0_attn_a_in['w1'], 'L0_attn_a_b1': _L0_attn_a_in['b1'], 'L0_attn_a_w2': _L0_attn_a_in['w2'], 'L0_attn_a_b2': _L0_attn_a_in['b2'], 'L0_attn_b_Wq': _L0_attn_b_in['Wq'], 'L0_attn_b_bq': _L0_attn_b_in['bq'], 'L0_attn_b_Wk': _L0_attn_b_in['Wk'], 'L0_attn_b_bk': _L0_attn_b_in['bk'], 'L0_attn_b_Wv': _L0_attn_b_in['Wv'], 'L0_attn_b_bv': _L0_attn_b_in['bv'], 'L0_attn_b_Wo': _L0_attn_b_in['Wo'], 'L0_attn_b_bo': _L0_attn_b_in['bo'], 'L0_ffn_W1': _L0_ffn_in['W1'], 'L0_ffn_W2': _L0_ffn_in['W2'], 'L0_ffn_Wr': _L0_ffn_in['Wr']}
    _x0 = _d['L0_attn_a_hidden_states']
    _d['L0_attn_a_hidden_states'] = jax.random.normal(jax.random.fold_in(jax.random.key(seed), 1), (4, 512, 128), dtype=_x0.dtype)
    del _x0
    return _d

def reference(L0_attn_a_hidden_states, L0_attn_a_ln1_g, L0_attn_a_ln1_b, L0_attn_a_wq, L0_attn_a_bq, L0_attn_a_wk, L0_attn_a_bk, L0_attn_a_wv, L0_attn_a_bv, L0_attn_a_wproj, L0_attn_a_bproj, L0_attn_a_ln2_g, L0_attn_a_ln2_b, L0_attn_a_w1, L0_attn_a_b1, L0_attn_a_w2, L0_attn_a_b2, L0_attn_b_Wq, L0_attn_b_bq, L0_attn_b_Wk, L0_attn_b_bk, L0_attn_b_Wv, L0_attn_b_bv, L0_attn_b_Wo, L0_attn_b_bo, L0_ffn_W1, L0_ffn_W2, L0_ffn_Wr):

    def _L0_attn_a_ref(hidden_states, ln1_g, ln1_b, wq, bq, wk, bk, wv, bv, wproj, bproj, ln2_g, ln2_b, w1, b1, w2, b2):
        import jax, jax.numpy as jnp
        import numpy as np
        HID = 128
        NH = 16
        HD = HID // NH
        WIN = 64
        EPS = 1e-05

        def layernorm(x, g, b):
            m = jnp.mean(x, axis=-1, keepdims=True)
            v = jnp.mean((x - m) ** 2, axis=-1, keepdims=True)
            return (x - m) / jnp.sqrt(v + EPS) * g + b

        def windowed_attention(q, k, v, window_size):
            bh, S, D = q.shape
            scale = float(D) ** (-0.5)
            w2, w4 = (window_size // 2, window_size // 4)
            out = jnp.zeros_like(q)
            for i in range(0, S, w2):
                start = max(0, i - w4)
                end = min(S, i + window_size - w4)
                qw = q[:, start:end] * scale
                kw = k[:, start:end]
                vw = v[:, start:end]
                attn = jax.nn.softmax(jnp.einsum('bqd,bkd->bqk', qw, kw), axis=-1)
                wo = jnp.einsum('bqk,bkd->bqd', attn, vw)
                if i == 0:
                    out = out.at[:, start:end].set(wo)
                else:
                    oe = min(i + w4, S)
                    n = oe - start
                    alphas = jnp.linspace(0.0, 1.0, n).reshape(1, -1, 1)
                    blended = (1 - alphas) * out[:, start:oe] + alphas * wo[:, :n]
                    out = out.at[:, start:oe].set(blended)
                    out = out.at[:, oe:end].set(wo[:, n:end - start])
            return out
        B, S, _ = hidden_states.shape
        residual = hidden_states
        x = layernorm(hidden_states, ln1_g, ln1_b)
        q = (x @ wq + bq).reshape(B, S, NH, HD).transpose(0, 2, 1, 3).reshape(B * NH, S, HD)
        k = (x @ wk + bk).reshape(B, S, NH, HD).transpose(0, 2, 1, 3).reshape(B * NH, S, HD)
        v = (x @ wv + bv).reshape(B, S, NH, HD).transpose(0, 2, 1, 3).reshape(B * NH, S, HD)
        ctx = windowed_attention(q, k, v, WIN)
        ctx = ctx.reshape(B, NH, S, HD).transpose(0, 2, 1, 3).reshape(B, S, HID)
        out = ctx @ wproj + bproj + residual
        residual2 = out
        h = layernorm(out, ln2_g, ln2_b)
        h = jax.nn.gelu(h @ w1 + b1, approximate=False)
        h = h @ w2 + b2
        return h + residual2

    def _L0_attn_b_ref(x, Wq, bq, Wk, bk, Wv, bv, Wo, bo):
        import jax, jax.numpy as jnp
        import numpy as np
        D_MODEL = 128
        N_HEADS = 16
        HEAD_DIM = D_MODEL // N_HEADS
        WINDOW = 128

        def _window_starts(seq_len, window):
            starts = []
            for i in range(0, seq_len, window // 2):
                end = min(i + window, seq_len)
                starts.append(max(0, end - window))
                if end == seq_len:
                    break
            return np.asarray(starts, dtype=np.int32)
        B, S, D = x.shape
        q = x @ Wq + bq
        k = x @ Wk + bk
        v = x @ Wv + bv
        starts = _window_starts(S, WINDOW)
        idx = starts[:, None] + np.arange(WINDOW)[None, :]
        idx_j = jnp.asarray(idx)
        qw = q[:, idx_j]
        kw = k[:, idx_j]
        vw = v[:, idx_j]
        scores = jnp.einsum('bwqd,bwkd->bwqk', qw, kw) / np.sqrt(HEAD_DIM)
        attn = jax.nn.softmax(scores, axis=-1)
        out_w = jnp.einsum('bwqk,bwkd->bwqd', attn, vw)
        flat_idx = idx.reshape(-1)
        out = jnp.zeros((B, S, D), x.dtype).at[:, flat_idx].add(out_w.reshape(B, -1, D))
        counts = jnp.zeros((S,), x.dtype).at[flat_idx].add(1.0)
        out = out / counts[None, :, None]
        return out @ Wo + bo

    def _L0_ffn_ref(x, W1, W2, Wr):
        import jax, jax.numpy as jnp
        import numpy as np
        B, T, D = (2, 256, 128)
        E, DFF, TOPK = (8, 512, 2)
        TEMPERATURE = 1.0
        logits = jnp.einsum('btd,ed->bte', x, Wr)
        probs = jax.nn.softmax(logits / TEMPERATURE, axis=-1)
        topk_vals, topk_idx = jax.lax.top_k(probs, TOPK)
        router_weights = topk_vals / topk_vals.sum(-1, keepdims=True)
        one_hot = jax.nn.one_hot(topk_idx, E, dtype=x.dtype)
        gate = jnp.einsum('btk,btke->bte', router_weights, one_hot)
        h = jax.nn.silu(jnp.einsum('btd,efd->btef', x, W1))
        y = jnp.einsum('btef,edf->bted', h, W2)
        out = jnp.einsum('bte,bted->btd', gate, y)
        return out
    x = L0_attn_a_hidden_states
    x = x + _L0_attn_a_ref(_layernorm(x, axis=-1), L0_attn_a_ln1_g, L0_attn_a_ln1_b, L0_attn_a_wq, L0_attn_a_bq, L0_attn_a_wk, L0_attn_a_bk, L0_attn_a_wv, L0_attn_a_bv, L0_attn_a_wproj, L0_attn_a_bproj, L0_attn_a_ln2_g, L0_attn_a_ln2_b, L0_attn_a_w1, L0_attn_a_b1, L0_attn_a_w2, L0_attn_a_b2)
    x = x + _L0_ffn_ref(_layernorm(x, axis=-1), L0_ffn_W1, L0_ffn_W2, L0_ffn_Wr)
    x = x + _L0_attn_b_ref(_layernorm(x, axis=-1), L0_attn_b_Wq, L0_attn_b_bq, L0_attn_b_Wk, L0_attn_b_bk, L0_attn_b_Wv, L0_attn_b_bv, L0_attn_b_Wo, L0_attn_b_bo)
    x = x + _L0_ffn_ref(_layernorm(x, axis=-1), L0_ffn_W1, L0_ffn_W2, L0_ffn_Wr)
    return x

_drawn_inputs = setup_inputs


def setup_inputs(seed=0):
    import zlib

    import numpy as np

    out = dict(_drawn_inputs(seed))
    spreads = {'L0_attn_a_ln1_g': (1.0, 0.6),
     'L0_attn_a_ln1_b': (0.0, 0.8),
     'L0_attn_a_bq': (0.0, 0.8),
     'L0_attn_a_bk': (0.0, 2.0),
     'L0_attn_a_bv': (0.0, 0.494),
     'L0_attn_a_bproj': (0.0, 0.1),
     'L0_attn_a_ln2_g': (1.0, 0.6),
     'L0_attn_a_ln2_b': (0.0, 2.0),
     'L0_attn_a_b1': (0.0, 0.532),
     'L0_attn_a_b2': (0.0, 0.1)}
    factors = {'L0_attn_a_wq': 8.0,
     'L0_attn_a_wk': 8.0,
     'L0_attn_a_wv': 8.0,
     'L0_attn_a_wproj': 3.256,
     'L0_attn_b_bq': 5.339,
     'L0_attn_b_bk': 64.0,
     'L0_attn_b_bv': 4.938,
     'L0_attn_b_bo': 5.557}
    for name, (base, spread) in spreads.items():
        noise = np.random.default_rng([zlib.crc32(name.encode()), seed]).standard_normal(out[name].shape)
        drawn = base * np.exp(spread * noise) if base else spread * noise
        out[name] = jnp.asarray(drawn.astype(out[name].dtype))
    for name, factor in factors.items():
        out[name] = (out[name] * factor).astype(out[name].dtype)
    return out
```

```python
from contextlib import ExitStack

import numpy as np

import concourse.bass as bass
from concourse import mybir

F32 = mybir.dt.float32
BF16 = mybir.dt.bfloat16
ALU = mybir.AluOpType
ACT = mybir.ActivationFunctionType
AXX = mybir.AxisListType.X

P = 128
B, S, D = 4, 512, 128
NT = B * S // P
TB = S // P
EPS = 1e-5

NH, HD, WIN = 16, 8, 64
STEP = WIN // 2
PAD = WIN // 4
SP_ = S + 2 * PAD
HALF = SP_ // 2
NG = 4
PIECES = 4
NPAIR = NH // 2
UNITS = [(k, odd) for k in range(TB) for odd in range(2)]
C0 = [P * k + STEP * odd for k, odd in UNITS]
NU = len(UNITS)
VW = HD + 1
SCALE_A = float(HD) ** -0.5

NW = (S - P) // (P // 2) + 1
SCALE_B = float(1.0 / np.sqrt(8))

NE, DFF = 8, 512
KF = DFF // P
DA = 4 * D
FA = DA // P

COLS = {}
for _n, _w in (("ident", P), ("i64", WIN), ("wone", P), ("mq", 1), ("mk", 1), ("valid", NU), ("ones", 2 * NU),
               ("blend", 2 * NU), ("cnt", NW), ("lower", NE * NE)):
    COLS[_n] = (sum(w for _, w in COLS.values()), _w)
NC_ = sum(w for _, w in COLS.values())

PRIMED = {
    "tensor": ["a_st", "a_o", "f_lg_ps", "b_v_ps", "b_o", "b_pt_ps", "a_ct_ps", "f_xt_ps"],
    "scalar": ["a_ct", "a_pf", "f_hh", "b_p", "b_v", "b_pt"],
    "vector": ["a_nm", "a_c", "f_fl", "f_lg", "b_x", "a_qk", "a_ctx"],
    "gpsimd": ["a_r"],
}


def constants():
    c = {n: np.zeros((P, w), np.float32) for n, (_, w) in COLS.items()}
    r = np.arange(P)
    c["ident"][:] = np.eye(P)
    c["i64"][:] = r[:, None] % WIN == np.arange(WIN)[None]
    c["wone"][:] = r[:, None] // WIN == r[None] // WIN
    piece = r % 32 // HD
    c["mq"][:, 0] = -1.0 * (piece >= 2)
    c["mk"][:, 0] = -1.0 * (piece % 2)
    alpha = np.linspace(0.0, 1.0, STEP).astype(np.float32)
    for u, c0 in enumerate(C0):
        pos = c0 + r - PAD
        c["valid"][:, u] = (pos >= 0) & (pos < S)
        for w in range(2):
            c["ones"][:, NU * w + u] = c["valid"][:, u] * (r // WIN == w)
            j = (c0 + WIN * w) // STEP
            q = r % WIN
            a = np.where(q < STEP, alpha[q % STEP], 1 - alpha[q % STEP])
            if j == 0:
                a = np.where(q < STEP, 1.0, a)
            if j == S // STEP - 1:
                a = np.where(q >= STEP, 1.0, a)
            c["blend"][:, 2 * u + w] = a
    for w in range(NW):
        pos = w * P // 2 + r
        c["cnt"][:, w] = np.where((pos < P // 2) | (pos >= S - P // 2), 1.0, 0.5)
    c["lower"][:] = (np.arange(NE)[None] < np.arange(NE)[:, None]).reshape(1, -1)
    return np.concatenate([c[n] for n in COLS], axis=1)


class Steps:

    def __init__(self, eng, sem, per, base=0):
        self.eng, self.sem, self.per, self.base, self.n = eng, sem, per, base, 0

    def begin(self, turn):
        self.turn, self.n = turn, 0

    def did(self, ins):
        ins.then_inc(self.sem, 1)
        self.n += 1

    def settle(self):
        self.eng.wait_ge(self.sem, self.turn * self.per + self.base + self.n)

    def end(self):
        assert self.n == self.per, (self.sem, self.n)


def program(nc, a, out):
    ctx = ExitStack()
    with ctx:
        def sb(name, shape, dt=F32):
            return ctx.enter_context(nc.sbuf_tensor(name, shape, dt))

        def sem(name):
            return ctx.enter_context(nc.semaphore(name))

        PS = ctx.enter_context(nc.psum_tensor("PS", [P, 8, 512], F32))
        X = sb("X", [P, NT, D])
        CST = sb("CST", [P, NC_])

        def cst(name):
            o, w = COLS[name]
            return CST[:, o:o + w]

        ident = cst("ident")
        WQ, WK, WV = sb("WQ", [P, D]), sb("WK", [P, D]), sb("WV", [P, D])
        WP = sb("WP", [64, 2, D])
        W1A, W2A = sb("W1A", [P, DA]), sb("W2A", [P, FA, D])
        COLA = sb("COLA", [P, 4])
        B1A = sb("B1A", [P, FA])
        ROWS = sb("ROWS", [1, 5, D])
        BVA = sb("BVA", [64, 2])
        WQB, WKB, WVB, WOB = (sb(n, [P, D]) for n in ("WQB", "WKB", "WVB", "WOB"))
        COLB = sb("COLB", [P, 3])
        WRN, WRT = sb("WRN", [NE, D]), sb("WRT", [P, NE])
        W1R, W2R = sb("W1R", [P, NE * KF, D]), sb("W2R", [P, NE, DFF])
        WA = sb("WA", [P, 2, NE, DFF], BF16)
        WB = sb("WB", [P, 2, NE, KF, D], BF16)
        ONES = sb("ONES", [1, P])
        WQK3 = sb("WQK3", [P, 2, NG, PIECES * 32])
        BQK3R = sb("BQK3R", [1, 2, NG, PIECES * 32])
        BQK3 = sb("BQK3", [P, 2, NG])
        I64B, WONEB = sb("I64B", [P, WIN], BF16), sb("WONEB", [P, P], BF16)
        BIASROW = sb("BIASROW", [1, 2, D])
        ST6, T3, MV = sb("ST6", [P, TB, 6]), sb("T3", [P, 4, TB]), sb("MV", [P, TB, 2])
        SM, VE, NHALF = sb("SM", [P, 4, TB]), sb("VE", [P, TB]), sb("NHALF", [P, TB])
        XN, XZ = sb("XN", [P, TB, D]), sb("XZ", [P, TB, D])
        XT = sb("XT", [P, SP_])
        QF = sb("QF", [P, 2, HALF])
        HI = sb("HI", [P, 2, HALF], BF16)
        QK = sb("QK", [P, 2, NG, SP_], BF16)
        QKM = sb("QKM", [P, 2, NG, 4, SP_], BF16)
        VB = sb("VB", [P, NU, 2, NPAIR, 2, 2, VW], BF16)
        NM = sb("NM", [P, 2, NH])
        R = sb("R", [P, 2, NH, WIN], BF16)
        PH, PL = sb("PH", [P, 2, NH * WIN], BF16), sb("PL", [P, 2, NH * WIN], BF16)
        PF = sb("PF", [P, 2, NH * WIN])
        DEN = sb("DEN", [P, 2, 2, NPAIR])
        C = sb("C", [P, 2, 2, NPAIR * HD])
        CTE, CTO = sb("CTE", [64, 2, SP_]), sb("CTO", [64, 2, SP_])
        CT = sb("CT", [64, 2, S])
        RES2, HT = sb("RES2", [P, TB, D]), sb("HT", [P, S])
        H1 = sb("H1", [P, FA, S])
        FT = sb("FT", [P, S])
        FH, FL = (QKM[:, i].rearrange("p g h c -> p (g h c)")[:, 0:NT * P] for i in range(2))
        PR, PRE = sb("PR", [P, TB, NE]), sb("PRE", [P, TB, NE])
        GT, EQ = sb("GT", [P, TB, NE, NE]), sb("EQ", [P, TB, NE, NE])
        RK, SE = sb("RK", [P, TB, NE]), sb("SE", [P, TB, NE])
        GS = sb("GS", [P, 4, TB])
        GATE = sb("GATE", [P, NT, NE])
        HF = W1R[:].rearrange("p (c k a) d -> p c k (a d)", c=2, k=KF)
        HH, HL = (W2R[:, 4 * i:4 * i + 4, :].bitcast(BF16).rearrange("p (c a) (g s) -> p c (a g) s", c=2, s=S)
                  for i in range(2))
        QB, KB, OT = (H1[:, i, :] for i in range(3))
        VN, PN = (HT[:, 2 * D * i:2 * D * i + 2 * D].rearrange("p (c d) -> p c d", c=2) for i in range(2))
        BM, BS = sb("BM", [P, 2, 1]), sb("BS", [P, 2, 2])
        PT = RES2[:, 0:2, :]

        s = {n: sem(n) for n in (
            "ld_const", "ld_x", "ld_attn", "ld_moe", "ld_rows",
            "pool_consts", "ones_ready", "nhalf_ready", "bias_ps", "bias_ready",
            "wt_ps", "wt_hi", "wt_lo", "wr_ps", "wr_ready",
            "a_steps", "a_xz", "a_xt_ps", "a_xt", "a_qk_ps", "a_qf", "a_qk", "a_mask",
            "a_v_ps", "a_vh", "a_vl", "a_s", "a_nm", "a_r", "a_st", "a_ph", "a_pf", "a_pl",
            "a_o", "a_c", "a_ct_ps", "a_ct", "a_ctx", "a_proj_ps", "a_res2", "a_hz", "a_ht_ps",
            "a_ht", "a_h_ps", "a_h1", "a_y_ps", "a_x",
            "f_steps", "f_xz", "f_xt_ps", "f_ft", "f_fl", "f_lg_ps", "f_lg", "f_gate", "f_exp", "a_var", "a_rstd", "f_var", "f_rstd", "b_var", "b_rstd",
            "f_z", "f_hf", "f_hh", "f_hl", "f_y", "f_x",
            "b_steps", "b_xz", "b_xt_ps", "b_xt", "b_qk_ps", "b_qk", "b_s", "b_m", "b_p", "b_pn",
            "b_pt_ps", "b_pt", "b_v_ps", "b_v", "b_o", "b_oe", "b_ot", "b_y_ps", "b_x",
            "out_done")}

        ctx.enter_context(nc.allow_non_contiguous_dma(reason="small columns of biases"))
        block = ctx.enter_context(nc.Block())

        @block.sync
        def _(sp):
            def load(dst, src, name):
                sp.dma_start(dst, src).then_inc(s[name], 16)

            load(CST[:], a["cst"], "ld_const")
            xv = a["x"].rearrange("b (t p) d -> p (b t) d", p=P)
            load(X[:], xv, "ld_x")
            col = "(p o) -> p o"
            row = "(o d) -> o d"
            for i, n in enumerate(("bq", "bk", "bproj", "b2", "bo_b")):
                load(ROWS[:, i, :], a[n].rearrange(row, o=1), "ld_rows")
            load(BVA[:], a["bv"].rearrange("(h p) -> p h", h=2), "ld_rows")
            for i, n in enumerate(("ln1_g", "ln1_b", "ln2_g", "ln2_b")):
                load(COLA[:, i:i + 1], a[n].rearrange(col, o=1), "ld_rows")
            load(B1A[:], a["b1"].rearrange("(t p) -> p t", p=P), "ld_rows")
            for i, n in enumerate(("bq_b", "bk_b", "bv_b")):
                load(COLB[:, i:i + 1], a[n].rearrange(col, o=1), "ld_rows")
            load(WQ[:], a["wq"], "ld_attn")
            load(WK[:], a["wk"], "ld_attn")
            load(WV[:], a["wv"], "ld_attn")
            load(WP[:], a["wproj"].rearrange("(h p) n -> p h n", h=2), "ld_attn")
            load(W1A[:], a["w1"], "ld_attn")
            load(W2A[:], a["w2"].rearrange("(k p) n -> p k n", p=P), "ld_attn")
            for t, n in ((WQB, "Wq_b"), (WKB, "Wk_b"), (WVB, "Wv_b"), (WOB, "Wo_b")):
                load(t[:], a[n], "ld_attn")
            load(WRN[:], a["Wr"], "ld_moe")
            load(W1R[:], a["W1"].rearrange("e (k p) d -> p (e k) d", p=P), "ld_moe")
            load(W2R[:], a["W2"].rearrange("e d f -> d e f"), "ld_moe")
            sp.wait_ge(s["f_x"], 2 + 2 * NE * B)
            sp.dma_start(out.rearrange("b (t p) d -> p (b t) d", p=P), X[:]).then_inc(s["out_done"], 16)
            sp.wait_ge(s["out_done"], 16)

        LD_ROWS, LD_ATTN, LD_MOE = 16 * 14, 16 * 10, 16 * 3

        @block.gpsimd
        def _(pool):
            for name in PRIMED["gpsimd"]:
                pool.sem_inc(s[name], 1)
            nc.gpsimd.memset(NHALF[:], -0.5).then_inc(s["nhalf_ready"], 1)
            nc.gpsimd.memset(ONES[:], 1.0).then_inc(s["ones_ready"], 1)
            nc.gpsimd.memset(VB[:], 0.0).then_inc(s["pool_consts"], 1)
            nc.gpsimd.memset(QKM[:], 0.0).then_inc(s["pool_consts"], 1)
            nc.gpsimd.memset(CTE[:], 0.0).then_inc(s["pool_consts"], 1)
            nc.gpsimd.memset(CTO[:], 0.0).then_inc(s["pool_consts"], 1)
            pool.wait_ge(s["ld_const"], 16)
            nc.gpsimd.tensor_copy(I64B[:], cst("i64")).then_inc(s["pool_consts"], 1)
            nc.gpsimd.tensor_copy(WONEB[:], cst("wone")).then_inc(s["pool_consts"], 1)
            pool.wait_ge(s["ld_rows"], LD_ROWS)
            pool.wait_ge(s["ld_attn"], LD_ATTN)
            for m, w in enumerate((WQ, WK)):
                for hh in range(2):
                    for c in range(PIECES):
                        for src, dst in ((w[:, 64 * hh:64 * hh + 64], WQK3[:, m]),
                                         (ROWS[:, m, 64 * hh:64 * hh + 64], BQK3R[:, m])):
                            d = dst.rearrange("q g (pp h c d) -> q h c (g pp) d", pp=2, h=2, c=PIECES)
                            nc.gpsimd.tensor_copy(d[:, hh, c], src.rearrange("q (p d) -> q p d", d=HD)) \
                                .then_inc(s["pool_consts"], 1)
            pool.wait_ge(s["pool_consts"], 1)
            for w in range(2):
                o = VB[:, :, 0, :, :, w, HD].rearrange("q u p h -> q u (p h)")
                v = cst("ones")[:, NU * w:NU * w + NU].unsqueeze(2).to_broadcast([P, NU, NH])
                nc.gpsimd.tensor_copy(o, v).then_inc(s["pool_consts"], 1)

            def unit_bias(turn, u):
                buf = u % 2
                pool.wait_ge(s["a_nm"], 1 + turn * 2 * NU + 2 * u + 2)
                if u >= 2:
                    pool.wait_ge(s["a_st"], 1 + turn * 2 * NU + 2 * (u - 1))
                else:
                    pool.wait_ge(s["a_st"], 1 + turn * 2 * NU)
                nc.gpsimd.tensor_tensor(
                    R[:, buf], NM[:, buf].unsqueeze(2).to_broadcast([P, NH, WIN]),
                    I64B[:].unsqueeze(1).to_broadcast([P, NH, WIN]), ALU.mult).then_inc(s["a_r"], 1)

            def rstd(k, name, n):
                pool.wait_ge(s[name + "_var"], n)
                nc.gpsimd.tensor_tensor(SM[:, k, :], VE[:], NHALF[:], ALU.pow).then_inc(s[name + "_rstd"], 1)

            pool.wait_ge(s["nhalf_ready"], 1)
            with pool.Fori(0, B) as b:
                rstd(0, "a", b * 3 + 1)
                rstd(1, "a", b * 3 + 2)
                for u in range(NU):
                    unit_bias(b, u)
                rstd(0, "a", b * 3 + 3)
            with pool.Fori(0, B) as b:
                rstd(0, "f", b + 1)
            with pool.Fori(0, B) as b:
                rstd(0, "b", b + 1)
            with pool.Fori(0, B) as b:
                rstd(0, "f", b + B + 1)

        POOL_CONSTS = 6 + 2 * 2 * PIECES * 2 + 2
        NWT = 2 * NE

        @block.tensor
        def _(pe):
            mm = nc.tensor.matmul
            for name in PRIMED["tensor"]:
                pe.sem_inc(s[name], 1)

            def tr(dst, src, n=P):
                return nc.tensor.transpose(dst, src, ident[0:n, 0:n])

            pe.wait_ge(s["pool_consts"], POOL_CONSTS)
            pe.wait_ge(s["ones_ready"], 1)
            for m in range(2):
                for g in range(NG):
                    mm(PS[:, 7, m * NG + g:m * NG + g + 1], BQK3R[0:1, m, g, :], ONES[0:1, 0:1], start=True, stop=True)
            for hh in range(2):
                mm(PS[0:1, 6, 0:D], BVA[:, hh:hh + 1], WP[:, hh, :], start=hh == 0, stop=hh == 1)
            mm(PS[0:1, 6, D:2 * D], COLB[:, 2:3], WOB[:], start=True, stop=True).then_inc(s["bias_ps"], 1)
            pe.wait_ge(s["ld_moe"], LD_MOE)
            tr(PS[:, 5, 0:NE], WRN[:], NE).then_inc(s["wr_ps"], 1)
            for i in range(NWT):
                e, second = i // 2, i % 2
                if i >= 4:
                    pe.wait_ge(s["wt_lo"], i - 3)
                for k in range(KF):
                    src = W2R[:, e, k * P:k * P + P] if second else W1R[:, e * KF + k, :]
                    last = tr(PS[:, i % 4, k * P:k * P + P], src)
                last.then_inc(s["wt_ps"], 1)

            def attention_a(b):
                pe.wait_ge(s["a_xz"], (b + 1) * TB)
                pe.wait_ge(s["bias_ready"], 4)
                pe.wait_ge(s["a_ct"], 1 + b * 2 * NU)
                for j in range(TB):
                    last = tr(PS[:, 6, j * P:j * P + P], XZ[:, j, :])
                last.then_inc(s["a_xt_ps"], 1)
                pe.wait_ge(s["a_xt"], (b + 1) * 3)
                n = 0
                for m in range(2):
                    for g in range(NG):
                        for h in range(2):
                            if n >= 2:
                                pe.wait_ge(s["a_qf"], b * 16 + n - 1)
                            mm(PS[:, 6 + n % 2, 0:HALF], WQK3[:, m, g, :], XT[:, h * HALF:(h + 1) * HALF],
                               start=True, stop=True).then_inc(s["a_qk_ps"], 1)
                            n += 1

                def scores(u):
                    for k in range(2):
                        pe.wait_ge(s["a_nm"], 1 + b * 2 * NU + max(0, 2 * u + k - 1) if u else b * 2 * NU)
                        for g in (2 * k, 2 * k + 1):
                            for w in range(2):
                                c = C0[u] + WIN * w
                                o = PS[64 * w:64 * w + 64, k, (g % 2) * 256:(g % 2) * 256 + 256]
                                last = mm(o, QK[:, 0, g, c:c + WIN], QKM[:, 1, g, :, c:c + WIN],
                                          start=g % 2 == 0, stop=g % 2 == 1, skip_group_check=True)
                        last.then_inc(s["a_s"], 1)

                def values(u):
                    if u == 0:
                        pe.wait_ge(s["a_qf"], (b + 1) * 16)
                    else:
                        pe.wait_ge(s["a_vl"], b * 2 * NU + 2 * u)
                    mm(PS[:, 6, 0:D], XT[:, C0[u]:C0[u] + P], WV[:], start=True, stop=True) \
                        .then_inc(s["a_v_ps"], 1)

                def scores_t(u):
                    pe.wait_ge(s["a_r"], 1 + b * NU + u + 1)
                    for k in range(2):
                        pe.wait_ge(s["a_pf"], 1 + b * 2 * NU + (2 * (u - 1) + k + 1 if u else 0))
                        mm(PS[:, 2 + k, :], WONEB[:], R[:, u % 2, 8 * k:8 * k + 8, :], start=True, stop=False,
                           skip_group_check=True)
                        for g in (2 * k, 2 * k + 1):
                            for w in range(2):
                                c = C0[u] + WIN * w
                                o = PS[64 * w:64 * w + 64, 2 + k, (g % 2) * 256:(g % 2) * 256 + 256]
                                last = mm(o, QK[:, 1, g, c:c + WIN], QKM[:, 0, g, :, c:c + WIN],
                                          start=False, stop=True, skip_group_check=True)
                        last.then_inc(s["a_st"], 1)

                def weighted(u):
                    buf = u % 2
                    pe.wait_ge(s["a_pl"], b * 2 * NU + 2 * u + 2)
                    pe.wait_ge(s["a_vl"], b * 2 * NU + 2 * u + 2)
                    pe.wait_ge(s["a_c"], 1 + b * 4 * NU + (4 * (u - 1) if u >= 2 else 0))
                    n = 4 * VW
                    for p in range(NPAIR):
                        o = PS[:, 4 + buf, n * p:n * p + n]
                        vh = VB[:, u, 0, p].rearrange("q h w v -> q (h w v)")
                        vl = VB[:, u, 1, p].rearrange("q h w v -> q (h w v)")
                        mm(o, PH[:, buf, P * p:P * p + P], vh, start=True, stop=False)
                        mm(o, PH[:, buf, P * p:P * p + P], vl, start=False, stop=False)
                        last = mm(o, PL[:, buf, P * p:P * p + P], vh, start=False, stop=True)
                    last.then_inc(s["a_o"], 1)

                def context_t(u):
                    pe.wait_ge(s["a_c"], 1 + b * 4 * NU + 4 * (u + 1))
                    pe.wait_ge(s["a_ct"], 1 + b * 2 * NU + 2 * u)
                    tr(PS[:, 7, 0:P], C[:, u % 2].rearrange("q w c -> q (w c)")).then_inc(s["a_ct_ps"], 1)

                pe.wait_ge(s["a_mask"], (b + 1) * 8)
                for t in range(NU + 3):
                    if t < NU:
                        scores(t)
                        values(t)
                    if 1 <= t <= NU:
                        scores_t(t - 1)
                    if 2 <= t <= NU + 1:
                        weighted(t - 2)
                    if 3 <= t:
                        context_t(t - 3)

                pe.wait_ge(s["a_ctx"], 1 + b + 1)
                for j in range(TB):
                    o = PS[:, 6, j * D:j * D + D]
                    mm(o, ONES[:], BIASROW[:, 0, :], start=True, stop=False)
                    for hh in range(2):
                        last = mm(o, CT[:, hh, j * P:j * P + P], WP[:, hh, :], start=False, stop=hh == 1)
                last.then_inc(s["a_proj_ps"], 1)
                pe.wait_ge(s["a_hz"], (b + 1) * TB)
                for j in range(TB):
                    last = tr(PS[:, 7, j * P:j * P + P], XZ[:, j, :])
                last.then_inc(s["a_ht_ps"], 1)
                pe.wait_ge(s["a_ht"], b + 1)
                for f in range(FA):
                    mm(PS[:, f, :], W1A[:, f * P:f * P + P], HT[:], start=True, stop=True).then_inc(s["a_h_ps"], 1)
                pe.wait_ge(s["a_h1"], (b + 1) * FA)
                for j in range(TB):
                    o = PS[:, 4, j * D:j * D + D]
                    mm(o, ONES[:], ROWS[:, 3, :], start=True, stop=False)
                    for k in range(FA):
                        last = mm(o, H1[:, k, j * P:j * P + P], W2A[:, k, :], start=False, stop=k == FA - 1)
                last.then_inc(s["a_y_ps"], 1)

            with pe.Fori(0, B) as b:
                attention_a(b)

            def experts(f):
                def route(b):
                    i = b + B * f
                    pe.wait_ge(s["f_xz"], (i + 1) * TB)
                    pe.wait_ge(s["f_fl"], 1 + i)
                    for j in range(TB):
                        last = tr(PS[:, 6, j * P:j * P + P], XZ[:, j, :])
                    last.then_inc(s["f_xt_ps"], 1)
                    pe.wait_ge(s["f_ft"], i + 1)
                    pe.wait_ge(s["f_lg"], 1 + i)
                    for j in range(TB):
                        last = mm(PS[:, 7, j * NE:j * NE + NE], FT[:, j * P:j * P + P], WRT[:], start=True, stop=True)
                    last.then_inc(s["f_lg_ps"], 1)

                with pe.Fori(0, B) as b:
                    route(b)
                pe.wait_ge(s["f_gate"], B * (f + 1))
                pe.wait_ge(s["f_fl"], 1 + B * (f + 1))

                def hidden(e, c):
                    i = f * NE * B + e * B + c
                    for k in range(KF):
                        if isinstance(e, int) and e == 0 and c == 0:
                            pe.wait_ge(s["f_hh"], 1 + f * NE * B * KF)
                        else:
                            pe.wait_ge(s["f_hh"], 1 + i * KF - KF + k + 1)
                        o = PS[:, k, :]
                        wh, wl = WA[:, 0, e, k * P:k * P + P], WA[:, 1, e, k * P:k * P + P]
                        xh, xl = FH[:, c * S:c * S + S], FL[:, c * S:c * S + S]
                        mm(o, wh, xh, start=True, stop=False)
                        mm(o, wh, xl, start=False, stop=False)
                        mm(o, wl, xh, start=False, stop=True).then_inc(s["f_z"], 1)

                def outputs(e, c):
                    i = f * NE * B + e * B + c
                    pe.wait_ge(s["f_hl"], (i + 1) * KF)
                    pe.wait_ge(s["f_x"], i + 1)
                    for j in range(TB):
                        o = PS[:, 4 + c % 2, j * D:j * D + D]
                        for k in range(KF):
                            hh, hl = HH[:, c % 2, k, j * P:j * P + P], HL[:, c % 2, k, j * P:j * P + P]
                            mm(o, hh, WB[:, 0, e, k, :], start=k == 0, stop=False)
                            mm(o, hh, WB[:, 1, e, k, :], start=False, stop=False)
                            last = mm(o, hl, WB[:, 0, e, k, :], start=False, stop=k == KF - 1)
                    last.then_inc(s["f_y"], 1)

                hidden(0, 0)
                with pe.Fori(0, NE - 1) as e:
                    for c in range(B):
                        hidden(e if c < B - 1 else e + 1, (c + 1) % B)
                        outputs(e, c)
                for c in range(B):
                    if c < B - 1:
                        hidden(NE - 1, c + 1)
                    outputs(NE - 1, c)

            pe.wait_ge(s["wr_ready"], 1)
            pe.wait_ge(s["a_x"], B)
            experts(0)

            def attention_b(b):
                pe.wait_ge(s["b_xz"], (b + 1) * TB)
                for j in range(TB):
                    last = tr(PS[:, 6, j * P:j * P + P], XZ[:, j, :])
                last.then_inc(s["b_xt_ps"], 1)
                pe.wait_ge(s["b_xt"], b + 1)
                pe.wait_ge(s["b_x"], 1 + b)
                mm(PS[:, 7, :], WQB[:], FT[:], start=True, stop=True).then_inc(s["b_qk_ps"], 1)
                mm(PS[:, 0, :], WKB[:], FT[:], start=True, stop=True).then_inc(s["b_qk_ps"], 1)
                pe.wait_ge(s["b_qk"], (b + 1) * 2)

                def scores(w):
                    c = w * P // 2
                    pe.wait_ge(s["b_p"], 1 + b * NW + (w - 1 if w >= 2 else 0))
                    mm(PS[:, 1 + w % 2, 0:P], QB[:, c:c + P], KB[:, c:c + P], start=True, stop=True) \
                        .then_inc(s["b_s"], 1)
                    pe.wait_ge(s["b_v"], 1 + b * NW + w)
                    mm(PS[:, 3, 0:D], FT[:, c:c + P], WVB[:], start=True, stop=True).then_inc(s["b_v_ps"], 1)

                def weighted(w):
                    pe.wait_ge(s["b_pn"], b * NW + w + 1)
                    pe.wait_ge(s["b_pt"], 1 + b * NW + w)
                    tr(PS[:, 4, 0:P], PN[:, w % 2, :]).then_inc(s["b_pt_ps"], 1)
                    pe.wait_ge(s["b_pt"], 1 + b * NW + w + 1)
                    pe.wait_ge(s["b_v"], 1 + b * NW + w + 1)
                    c = w // 2 * P
                    mm(PS[:, 0 if w % 2 else 5, c:c + P], VN[:, w % 2, :], PT[:, w % 2, :], start=True, stop=True) \
                        .then_inc(s["b_o"], 1)

                for t in range(NW + 1):
                    if t < NW:
                        scores(t)
                    if t:
                        weighted(t - 1)
                pe.wait_ge(s["b_ot"], b + 1)
                for j in range(TB):
                    o = PS[:, 7, j * D:j * D + D]
                    mm(o, ONES[:], BIASROW[:, 1, :], start=True, stop=False)
                    last = mm(o, OT[:, j * P:j * P + P], WOB[:], start=False, stop=True)
                last.then_inc(s["b_y_ps"], 1)

            pe.wait_ge(s["f_x"], 2 + NE * B)
            with pe.Fori(0, B) as b:
                attention_b(b)
            pe.wait_ge(s["b_x"], 1 + B)
            experts(1)

        @block.scalar
        def _(act):
            fn = nc.scalar.activation
            for name in PRIMED["scalar"]:
                act.sem_inc(s[name], 1)
            act.wait_ge(s["bias_ps"], 1)
            fn(BQK3[:, 0, :], PS[:, 7, 0:NG], ACT.Copy, scale=SCALE_A).then_inc(s["bias_ready"], 1)
            fn(BQK3[:, 1, :], PS[:, 7, NG:2 * NG], ACT.Copy).then_inc(s["bias_ready"], 1)
            act.wait_ge(s["wr_ps"], 1)
            fn(WRT[:], PS[:, 5, 0:NE], ACT.Copy).then_inc(s["wr_ready"], 1)
            for i in range(NWT):
                e, second = i // 2, i % 2
                act.wait_ge(s["wt_ps"], i + 1)
                o = WB[:, 0, e].rearrange("p k d -> p (k d)") if second else WA[:, 0, e, :]
                fn(o, PS[:, i % 4, :], ACT.Copy).then_inc(s["wt_hi"], 1)

            def attention_a(b):
                act.wait_ge(s["a_xt_ps"], b + 1)
                act.wait_ge(s["ld_rows"], LD_ROWS)
                fn(XT[:, PAD:PAD + S], PS[:, 6, :], ACT.Identity, scale=COLA[:, 0:1], bias=COLA[:, 1:2]) \
                    .then_inc(s["a_xt"], 1)
                for dst, src in ((0, 0), (PAD + S, S - PAD)):
                    fn(XT[:, dst:dst + PAD], PS[:, 6, src:src + PAD], ACT.Identity, scale=COLA[:, 0:1],
                       bias=COLA[:, 1:2]).then_inc(s["a_xt"], 1)
                n = 0
                for m in range(2):
                    for g in range(NG):
                        for h in range(2):
                            act.wait_ge(s["a_qk_ps"], b * 16 + n + 1)
                            act.wait_ge(s["a_qk"], 1 + b * 16 + (n - 1 if n >= 2 else 0))
                            fn(QF[:, n % 2, :], PS[:, 6 + n % 2, 0:HALF], ACT.Identity,
                               scale=SCALE_A if m == 0 else 1.0, bias=BQK3[:, m, g:g + 1]).then_inc(s["a_qf"], 1)
                            n += 1

                def values_hi(u):
                    act.wait_ge(s["a_v_ps"], b * NU + u + 1)
                    for w in range(2):
                        rows = slice(64 * w, 64 * w + 64)
                        for hh in range(2):
                            fn(VB[rows, u, 0, :, hh, w, 0:HD],
                               PS[rows, 6, 64 * hh:64 * hh + 64].rearrange("q (p d) -> q p d", d=HD), ACT.Copy,
                               scale=cst("valid")[rows, u:u + 1]).then_inc(s["a_vh"], 1)

                def exponentials(u):
                    buf = u % 2
                    act.wait_ge(s["a_o"], 1 + b * NU + (u - 1 if u >= 2 else 0))
                    for k in range(2):
                        act.wait_ge(s["a_st"], 1 + b * 2 * NU + 2 * u + k + 1)
                        half = slice(512 * k, 512 * k + 512)
                        fn(PH[:, buf, half], PS[:, 2 + k, :], ACT.Exp).then_inc(s["a_ph"], 1)
                        fn(PF[:, buf, half], PS[:, 2 + k, :], ACT.Exp).then_inc(s["a_pf"], 1)

                def context_out(u):
                    k, odd = UNITS[u]
                    act.wait_ge(s["a_ct_ps"], 1 + b * NU + u + 1)
                    for w in range(2):
                        c = C0[u] + WIN * w
                        fn((CTO if odd else CTE)[:, :, c:c + WIN],
                           PS[64 * w:64 * w + 64, 7, 0:P].rearrange("c (h q) -> c h q", h=2), ACT.Copy) \
                            .then_inc(s["a_ct"], 1)

                act.wait_ge(s["a_ctx"], 1 + b)
                for t in range(NU + 3):
                    if t < NU:
                        values_hi(t)
                    if 1 <= t <= NU:
                        exponentials(t - 1)
                    if 3 <= t:
                        context_out(t - 3)
                act.wait_ge(s["a_ht_ps"], b + 1)
                fn(HT[:], PS[:, 7, :], ACT.Identity, scale=COLA[:, 2:3], bias=COLA[:, 3:4]).then_inc(s["a_ht"], 1)
                for k in range(FA):
                    act.wait_ge(s["a_h_ps"], b * FA + k + 1)
                    fn(H1[:, k, :], PS[:, k, :], ACT.Gelu, bias=B1A[:, k:k + 1]).then_inc(s["a_h1"], 1)

            with act.Fori(0, B) as b:
                attention_a(b)

            def experts(f):
                def route(b):
                    i = b + B * f
                    act.wait_ge(s["f_xt_ps"], 1 + i + 1)
                    act.wait_ge(s["f_lg_ps"], 1 + i)
                    act.wait_ge(s["f_fl"], 1 + i)
                    fn(FT[:], PS[:, 6, :], ACT.Copy).then_inc(s["f_ft"], 1)
                    act.wait_ge(s["f_lg"], 1 + i + 1)
                    fn(PRE[:], PR[:], ACT.Exp).then_inc(s["f_exp"], 1)

                with act.Fori(0, B) as b:
                    route(b)

                def silu(e, c):
                    i = f * NE * B + e * B + c
                    for k in range(KF):
                        act.wait_ge(s["f_z"], i * KF + k + 1)
                        if isinstance(e, int) and e == 0 and c < 2:
                            act.wait_ge(s["f_y"], f * NE * B)
                        else:
                            act.wait_ge(s["f_y"], i - 1)
                        fn(HF[:, c % 2, k, :], PS[:, k, :], ACT.Silu).then_inc(s["f_hf"], 1)
                        fn(HH[:, c % 2, k, :], PS[:, k, :], ACT.Silu).then_inc(s["f_hh"], 1)

                for c in range(2):
                    silu(0, c)
                with act.Fori(0, NE - 1) as e:
                    for c in range(B):
                        silu(e if c < B - 2 else e + 1, (c + 2) % B)
                for c in range(2):
                    silu(NE - 1, c + 2)

            experts(0)

            def attention_b(b):
                act.wait_ge(s["b_xt_ps"], b + 1)
                act.wait_ge(s["b_v_ps"], 1 + b * NW)
                fn(FT[:], PS[:, 6, :], ACT.Copy).then_inc(s["b_xt"], 1)
                for m, (dst, bank) in enumerate(((QB, 7), (KB, 0))):
                    act.wait_ge(s["b_qk_ps"], b * 2 + m + 1)
                    fn(dst, PS[:, bank, :], ACT.Identity, bias=COLB[:, m:m + 1]).then_inc(s["b_qk"], 1)

                def softmax(w):
                    act.wait_ge(s["b_v_ps"], 1 + b * NW + w + 1)
                    act.wait_ge(s["b_o"], 1 + b * NW + (w - 1 if w >= 2 else 0))
                    fn(VN[:, w % 2, :], PS[:, 3, 0:D], ACT.Copy).then_inc(s["b_v"], 1)
                    act.wait_ge(s["b_m"], b * NW + w + 1)
                    act.wait_ge(s["b_pt_ps"], 1 + b * NW + (w - 1 if w >= 2 else 0))
                    fn(PN[:, w % 2, :], PS[:, 1 + w % 2, 0:P], ACT.Exp, scale=SCALE_B, bias=BM[:, w % 2, :],
                       accum_out=BS[:, w % 2, 0:1]).then_inc(s["b_p"], 1)

                def transposed(w):
                    act.wait_ge(s["b_pt_ps"], 1 + b * NW + w + 1)
                    fn(PT[:, w % 2, :], PS[:, 4, 0:P], ACT.Copy).then_inc(s["b_pt"], 1)

                for t in range(NW + 1):
                    if t < NW:
                        softmax(t)
                    if t:
                        transposed(t - 1)

            with act.Fori(0, B) as b:
                attention_b(b)
            experts(1)

        @block.vector
        def _(dve):
            v = nc.vector
            for name in PRIMED["vector"]:
                dve.sem_inc(s[name], 1)
            dve.sem_inc(s["f_x"], 2)
            dve.wait_ge(s["bias_ps"], 1)
            dve.wait_ge(s["bias_ready"], 2)
            for i, r in enumerate((2, 4)):
                v.tensor_tensor(BIASROW[:, i, :], PS[0:1, 6, D * i:D * i + D], ROWS[:, r, :], ALU.add) \
                    .then_inc(s["bias_ready"], 1)
            for i in range(NWT):
                e, second = i // 2, i % 2
                dve.wait_ge(s["wt_hi"], i + 1)
                hi = WB[:, 0, e].rearrange("p k d -> p (k d)") if second else WA[:, 0, e, :]
                lo = WB[:, 1, e].rearrange("p k d -> p (k d)") if second else WA[:, 1, e, :]
                v.tensor_tensor(lo, PS[:, i % 4, :], hi, ALU.subtract).then_inc(s["wt_lo"], 1)
            dve.wait_ge(s["ld_x"], 16)

            def stats(st, tile, var, n):
                for j in range(TB):
                    st.did(v.bn_stats(ST6[:, j, :], tile(j)))
                st.settle()
                st.did(v.tensor_tensor(T3[:, 0, :], ST6[:, :, 1], ST6[:, :, 4], ALU.add))
                st.did(v.tensor_tensor(T3[:, 1, :], ST6[:, :, 1], ST6[:, :, 4], ALU.subtract))
                st.did(v.tensor_tensor(T3[:, 2, :], ST6[:, :, 2], ST6[:, :, 5], ALU.add))
                st.settle()
                st.did(v.tensor_scalar(MV[:, :, 0], T3[:, 0, :], 0.5, None, ALU.mult))
                st.did(v.scalar_tensor_tensor(T3[:, 3, :], T3[:, 1, :], 0.25, T3[:, 1, :], ALU.mult, ALU.mult))
                st.settle()
                st.did(v.scalar_tensor_tensor(MV[:, :, 1], T3[:, 2, :], 1.0 / D, T3[:, 3, :], ALU.mult, ALU.add))
                st.settle()
                v.tensor_scalar(VE[:], MV[:, :, 1], EPS, None, ALU.add).then_inc(s[var], 1)
                dve.wait_ge(s[var.replace("var", "rstd")], n)

            def normalise(dst, tile, r, name):
                for j in range(TB):
                    v.tensor_scalar(dst[:, j, :], tile(j), MV[:, j, 0:1], SM[:, r, j:j + 1],
                                    ALU.subtract, ALU.mult).then_inc(s[name], 1)

            A_STEPS = 2 * (TB + 6) + 3 + TB + 16 + 3 * NU + 1
            st = Steps(dve, s["a_steps"], A_STEPS)

            def attention_a(b):
                st.begin(b)
                x_tile = lambda j: X[:, TB * b + j, :]
                stats(st, x_tile, "a_var", b * 3 + 1)
                st.did(v.tensor_tensor(SM[:, 1, :], MV[:, :, 1], SM[:, 0, :], ALU.mult))
                st.settle()
                st.did(v.tensor_tensor(SM[:, 2, :], SM[:, 1, :], SM[:, 0, :], ALU.mult))
                st.settle()
                v.tensor_scalar(VE[:], SM[:, 2, :], EPS, None, ALU.add).then_inc(s["a_var"], 1)
                dve.wait_ge(s["a_rstd"], b * 3 + 2)
                st.did(v.tensor_tensor(SM[:, 3, :], SM[:, 1, :], SM[:, 0, :], ALU.mult))
                st.settle()
                for j in range(TB):
                    st.did(v.tensor_scalar(XN[:, j, :], x_tile(j), MV[:, j, 0:1], SM[:, 0, j:j + 1],
                                           ALU.subtract, ALU.mult))
                normalise(XZ, x_tile, 3, "a_xz")
                n = 0
                for m in range(2):
                    for g in range(NG):
                        for h in range(2):
                            cols = slice(h * HALF, (h + 1) * HALF)
                            dve.wait_ge(s["a_qf"], b * 16 + n + 1)
                            st.did(v.tensor_copy(HI[:, n % 2, :], QF[:, n % 2, :]))
                            st.settle()
                            v.scalar_tensor_tensor(QK[:, m, g, cols], HI[:, n % 2, :], cst("mk" if m else "mq"),
                                                   QF[:, n % 2, :], ALU.mult, ALU.add).then_inc(s["a_qk"], 1)
                            n += 1
                dve.wait_ge(s["a_qk"], 1 + (b + 1) * 16)
                for m in range(2):
                    for i in range(4):
                        rows = slice(32 * i, 32 * i + 32)
                        v.tensor_copy(QKM[rows, m, :, i, :], QK[rows, m, :, :]).then_inc(s["a_mask"], 1)

                def maxima(u):
                    for k in range(2):
                        dve.wait_ge(s["a_s"], b * 2 * NU + 2 * u + k + 1)
                        dve.wait_ge(s["a_r"], 1 + b * NU + (u - 1 if u >= 2 else 0))
                        v.tensor_reduce(NM[:, u % 2, 8 * k:8 * k + 8],
                                        PS[:, k, :].rearrange("q (h c) -> q h c", c=WIN), op=ALU.max, axis=AXX,
                                        negate=True).then_inc(s["a_nm"], 1)

                def values_lo(u):
                    dve.wait_ge(s["a_vh"], b * 4 * NU + 4 * u + 4)
                    for w in range(2):
                        rows = slice(64 * w, 64 * w + 64)
                        for hh in range(2):
                            ins = v.scalar_tensor_tensor(
                                VB[rows, u, 1, :, hh, w, 0:HD],
                                PS[rows, 6, 64 * hh:64 * hh + 64].rearrange("q (p d) -> q p d", d=HD),
                                cst("valid")[rows, u:u + 1], VB[rows, u, 0, :, hh, w, 0:HD], ALU.mult, ALU.subtract)
                        ins.then_inc(s["a_vl"], 1)

                def probabilities_lo(u):
                    for k in range(2):
                        half = slice(512 * k, 512 * k + 512)
                        dve.wait_ge(s["a_pf"], 1 + b * 2 * NU + 2 * u + k + 1)
                        v.tensor_tensor(PL[:, u % 2, half], PF[:, u % 2, half], PH[:, u % 2, half], ALU.subtract) \
                            .then_inc(s["a_pl"], 1)

                def normalised(u):
                    buf = u % 2
                    dve.wait_ge(s["a_o"], 1 + b * NU + u + 1)
                    dve.wait_ge(s["a_ct_ps"], 1 + b * NU + (u - 1 if u >= 2 else 0))

                    def o(hh):
                        return PS[64 * hh:64 * hh + 64, 4 + buf, 0:4 * VW * NPAIR].rearrange(
                            "q (p h w v) -> q h w p v", p=NPAIR, h=2, w=2)[:, hh]
                    for hh in range(2):
                        rows = slice(64 * hh, 64 * hh + 64)
                        st.did(v.reciprocal(DEN[rows, buf], o(hh)[:, :, :, HD]))
                    st.settle()
                    bl = cst("blend")[:, 2 * u:2 * u + 2].unsqueeze(2).to_broadcast([P, 2, NPAIR])
                    st.did(v.tensor_tensor(DEN[:, buf], DEN[:, buf], bl, ALU.mult))
                    st.settle()
                    for hh in range(2):
                        rows = slice(64 * hh, 64 * hh + 64)
                        for w in range(2):
                            d = DEN[rows, buf, w].unsqueeze(2).to_broadcast([64, NPAIR, HD])
                            v.tensor_tensor(C[rows, buf, w].rearrange("q (p d) -> q p d", d=HD),
                                            o(hh)[:, w, :, 0:HD], d, ALU.mult).then_inc(s["a_c"], 1)

                for t in range(NU + 2):
                    if t < NU:
                        maxima(t)
                        values_lo(t)
                    if 1 <= t <= NU:
                        probabilities_lo(t - 1)
                    if 2 <= t:
                        normalised(t - 2)
                dve.wait_ge(s["a_ct"], 1 + (b + 1) * 2 * NU)
                v.tensor_tensor(CT[:], CTE[:, :, PAD:PAD + S], CTO[:, :, PAD:PAD + S], ALU.add) \
                    .then_inc(s["a_ctx"], 1)
                dve.wait_ge(s["a_proj_ps"], b + 1)
                st.did(v.tensor_tensor(RES2[:], PS[:, 6, :].rearrange("p (j d) -> p j d", d=D), XN[:], ALU.add))
                st.settle()
                res = lambda j: RES2[:, j, :]
                stats(st, res, "a_var", b * 3 + 3)
                normalise(XZ, res, 0, "a_hz")
                dve.wait_ge(s["a_y_ps"], b + 1)
                xs = X[:, bass.ds(TB * b, TB), :]
                v.tensor_tensor(RES2[:], PS[:, 4, :].rearrange("p (j d) -> p j d", d=D), RES2[:], ALU.add) \
                    .then_inc(s["a_res2"], 1)
                dve.wait_ge(s["a_res2"], b + 1)
                v.tensor_tensor(xs, xs, RES2[:], ALU.add).then_inc(s["a_x"], 1)
                dve.wait_ge(s["a_x"], b + 1)
                st.end()

            with dve.Fori(0, B) as b:
                attention_a(b)

            F_STEPS = TB + 6 + 9

            def experts(f):
                fs = Steps(dve, s["f_steps"], F_STEPS, base=f * B * F_STEPS)

                def route(b):
                    i = b + B * f
                    fs.begin(b)
                    x_tile = lambda j: X[:, TB * b + j, :]
                    stats(fs, x_tile, "f_var", i + 1)
                    dve.wait_ge(s["f_xt_ps"], 1 + i)
                    normalise(XZ, x_tile, 0, "f_xz")
                    dve.wait_ge(s["f_ft"], i + 1)
                    cols = bass.ds(S * b, S)
                    fs.did(v.tensor_copy(FH[:, cols], FT[:]))
                    fs.settle()
                    v.tensor_tensor(FL[:, cols], FT[:], FH[:, cols], ALU.subtract).then_inc(s["f_fl"], 1)
                    dve.wait_ge(s["f_lg_ps"], 1 + i + 1)
                    lg = PS[:, 7, 0:TB * NE].rearrange("p (j e) -> p j e", e=NE)
                    fs.did(v.tensor_reduce(GS[:, 0, :], lg, op=ALU.max, axis=AXX))
                    fs.settle()
                    v.tensor_tensor(PR[:], lg, GS[:, 0, :].unsqueeze(2).to_broadcast([P, TB, NE]), ALU.subtract) \
                        .then_inc(s["f_lg"], 1)
                    dve.wait_ge(s["f_lg"], 1 + i + 1)
                    for j in range(TB):
                        pe_ = PR[:, j, :].unsqueeze(2).to_broadcast([P, NE, NE])
                        po = PR[:, j, :].unsqueeze(1).to_broadcast([P, NE, NE])
                        v.tensor_tensor(GT[:, j], po, pe_, ALU.is_gt)
                        last = v.tensor_tensor(EQ[:, j], po, pe_, ALU.is_equal)
                    fs.did(last)
                    fs.settle()
                    low = cst("lower").unsqueeze(1).to_broadcast([P, TB, NE * NE])
                    fs.did(v.tensor_tensor(EQ[:].rearrange("p j a c -> p j (a c)"),
                                           EQ[:].rearrange("p j a c -> p j (a c)"), low, ALU.mult))
                    fs.settle()
                    fs.did(v.tensor_tensor(GT[:], GT[:], EQ[:], ALU.add))
                    fs.settle()
                    fs.did(v.tensor_reduce(RK[:], GT[:], op=ALU.add, axis=AXX))
                    fs.settle()
                    dve.wait_ge(s["f_exp"], i + 1)
                    fs.did(v.scalar_tensor_tensor(SE[:].rearrange("p j e -> p (j e)"), RK[:].rearrange("p j e -> p (j e)"),
                                                  1.5, PRE[:].rearrange("p j e -> p (j e)"), ALU.is_lt, ALU.mult))
                    fs.settle()
                    fs.did(v.tensor_reduce(GS[:, 1, :], SE[:], op=ALU.add, axis=AXX))
                    fs.settle()
                    fs.did(v.reciprocal(GS[:, 2, :], GS[:, 1, :]))
                    fs.settle()
                    v.tensor_tensor(GATE[:, bass.ds(TB * b, TB), :], SE[:],
                                    GS[:, 2, :].unsqueeze(2).to_broadcast([P, TB, NE]), ALU.mult).then_inc(s["f_gate"], 1)
                    fs.end()

                with dve.Fori(0, B) as b:
                    route(b)
                dve.wait_ge(s["f_gate"], B * (f + 1))

                def hidden_lo(e, c):
                    i = f * NE * B + e * B + c
                    for k in range(KF):
                        dve.wait_ge(s["f_hh"], 1 + i * KF + k + 1)
                        v.tensor_tensor(HL[:, c % 2, k, :], HF[:, c % 2, k, :], HH[:, c % 2, k, :], ALU.subtract) \
                            .then_inc(s["f_hl"], 1)

                def combine(e, c):
                    i = f * NE * B + e * B + c
                    dve.wait_ge(s["f_y"], i + 1)
                    for j in range(TB):
                        t = c * TB + j
                        last = v.scalar_tensor_tensor(X[:, t, :], PS[:, 4 + c % 2, j * D:j * D + D], GATE[:, t, gate_col(e)],
                                                      X[:, t, :], ALU.mult, ALU.add)
                    last.then_inc(s["f_x"], 1)

                def gate_col(e):
                    return bass.ds(e, 1)

                hidden_lo(0, 0)
                with dve.Fori(0, NE - 1) as e:
                    for c in range(B):
                        hidden_lo(e if c < B - 1 else e + 1, (c + 1) % B)
                        combine(e, c)
                for c in range(B):
                    if c < B - 1:
                        hidden_lo(NE - 1, c + 1)
                    combine(NE - 1, c)
                dve.wait_ge(s["f_x"], 2 + NE * B * (f + 1))

            experts(0)

            B_STEPS = TB + 6 + 2 * NW + 1
            bs = Steps(dve, s["b_steps"], B_STEPS)

            def attention_b(b):
                bs.begin(b)
                x_tile = lambda j: X[:, TB * b + j, :]
                stats(bs, x_tile, "b_var", b + 1)
                normalise(XZ, x_tile, 0, "b_xz")

                def row_max(w):
                    dve.wait_ge(s["b_s"], b * NW + w + 1)
                    dve.wait_ge(s["b_p"], 1 + b * NW + (w - 1 if w >= 2 else 0))
                    bs.did(v.tensor_reduce(BM[:, w % 2, :], PS[:, 1 + w % 2, 0:P], op=ALU.max, axis=AXX, negate=True))
                    bs.settle()
                    v.tensor_scalar(BM[:, w % 2, :], BM[:, w % 2, :], SCALE_B, None, ALU.mult).then_inc(s["b_m"], 1)

                def divide(w):
                    dve.wait_ge(s["b_p"], 1 + b * NW + w + 1)
                    bs.did(v.reciprocal(BS[:, w % 2, 1:2], BS[:, w % 2, 0:1]))
                    bs.settle()
                    v.tensor_scalar(PN[:, w % 2, :], PN[:, w % 2, :], BS[:, w % 2, 1:2], cst("cnt")[:, w:w + 1],
                                    ALU.mult, ALU.mult).then_inc(s["b_pn"], 1)

                for t in range(NW + 1):
                    if t < NW:
                        row_max(t)
                    if t:
                        divide(t - 1)
                dve.wait_ge(s["b_o"], 1 + (b + 1) * NW)
                bs.did(v.tensor_copy(OT, PS[:, 5, :]))
                bs.settle()
                mid = slice(P // 2, S - P // 2)
                v.tensor_tensor(OT[:, mid], OT[:, mid], PS[:, 0, 0:S - P], ALU.add).then_inc(s["b_ot"], 1)
                dve.wait_ge(s["b_y_ps"], b + 1)
                xs = X[:, bass.ds(TB * b, TB), :]
                v.tensor_tensor(xs, PS[:, 7, :].rearrange("p (j d) -> p j d", d=D), xs, ALU.add).then_inc(s["b_x"], 1)
                dve.wait_ge(s["b_x"], 1 + b + 1)
                bs.end()

            with dve.Fori(0, B) as b:
                attention_b(b)
            experts(1)


PREFIX = {"a": "L0_attn_a_", "b": "L0_attn_b_", "f": "L0_ffn_"}
INPUTS = [("x", "L0_attn_a_hidden_states")] \
    + [(n, "L0_attn_a_" + n) for n in ("ln1_g", "ln1_b", "wq", "bq", "wk", "bk", "wv", "bv", "wproj", "bproj",
                                       "ln2_g", "ln2_b", "w1", "b1", "w2", "b2")] \
    + [(n + "_b", "L0_attn_b_" + n) for n in ("Wq", "bq", "Wk", "bk", "Wv", "bv", "Wo", "bo")] \
    + [(n, "L0_ffn_" + n) for n in ("W1", "W2", "Wr")]


def kernel(**inputs):
    import concourse.bacc as bacc
    from concourse.bass_utils import run_bass_kernel_spmd

    nc = bacc.Bacc("TRN2", target_bir_lowering=False, num_devices=1)
    arrays, args = {}, {}
    for name, given in INPUTS:
        arr = np.ascontiguousarray(inputs[given])
        arrays["in_" + name] = arr
        args[name] = nc.dram_tensor("in_" + name, arr.shape, F32, kind="ExternalInput").ap()
    arrays["in_cst"] = constants()
    args["cst"] = nc.dram_tensor("in_cst", (P, NC_), F32, kind="ExternalInput").ap()
    out = nc.dram_tensor("out", (B, S, D), F32, kind="ExternalOutput").ap()
    program(nc, args, out)
    r = run_bass_kernel_spmd(nc, [arrays], core_ids=[0])
    return r.results[0]["out"]
```

```python
from contextlib import ExitStack

import numpy as np

import concourse.bass as bass
from concourse import mybir

F32 = mybir.dt.float32
BF16 = mybir.dt.bfloat16
ALU = mybir.AluOpType
ACT = mybir.ActivationFunctionType
AXX = mybir.AxisListType.X

P = 128
B, S, D = 4, 512, 128
NT = B * S // P
TB = S // P
EPS = 1e-5

NH, HD, WIN = 16, 8, 64
STEP = WIN // 2
PAD = WIN // 4
SP_ = S + 2 * PAD
HALF = SP_ // 2
NG = 4
PIECES = 4
NPAIR = NH // 2
UNITS = [(k, odd) for k in range(TB) for odd in range(2)]
C0 = [P * k + STEP * odd for k, odd in UNITS]
NU = len(UNITS)
VW = HD + 1
SCALE_A = float(HD) ** -0.5

NW = (S - P) // (P // 2) + 1
SCALE_B = float(1.0 / np.sqrt(8))

NE, DFF = 8, 512
KF = DFF // P
DA = 4 * D
FA = DA // P

COLS = {}
for _n, _w in (("ident", P), ("i64", WIN), ("wone", P), ("mq", 1), ("mk", 1), ("valid", NU), ("ones", 2 * NU),
               ("blend", 2 * NU), ("cnt", NW), ("lower", NE * NE)):
    COLS[_n] = (sum(w for _, w in COLS.values()), _w)
NC_ = sum(w for _, w in COLS.values())

PRIMED = {
    "tensor": ["a_st", "a_o", "a_proj_ps", "b_v_ps", "b_o", "b_pt_ps", "a_ct_ps"],
    "scalar": ["a_ct", "a_pf", "f_hh", "b_p", "b_v", "b_pt"],
    "vector": ["a_nm", "a_c", "b_x", "a_qk", "a_res2"],
    "gpsimd": ["a_r"],
}


def constants():
    c = {n: np.zeros((P, w), np.float32) for n, (_, w) in COLS.items()}
    r = np.arange(P)
    c["ident"][:] = np.eye(P)
    c["i64"][:] = r[:, None] % WIN == np.arange(WIN)[None]
    c["wone"][:] = r[:, None] // WIN == r[None] // WIN
    piece = r % 32 // HD
    c["mq"][:, 0] = -1.0 * (piece >= 2)
    c["mk"][:, 0] = -1.0 * (piece % 2)
    alpha = np.linspace(0.0, 1.0, STEP).astype(np.float32)
    for u, c0 in enumerate(C0):
        pos = c0 + r - PAD
        c["valid"][:, u] = (pos >= 0) & (pos < S)
        for w in range(2):
            c["ones"][:, NU * w + u] = c["valid"][:, u] * (r // WIN == w)
            j = (c0 + WIN * w) // STEP
            q = r % WIN
            a = np.where(q < STEP, alpha[q % STEP], 1 - alpha[q % STEP])
            if j == 0:
                a = np.where(q < STEP, 1.0, a)
            if j == S // STEP - 1:
                a = np.where(q >= STEP, 1.0, a)
            c["blend"][:, 2 * u + w] = a
    for w in range(NW):
        pos = w * P // 2 + r
        c["cnt"][:, w] = np.where((pos < P // 2) | (pos >= S - P // 2), 1.0, 0.5)
    c["lower"][:] = (np.arange(NE)[None] < np.arange(NE)[:, None]).reshape(1, -1)
    return np.concatenate([c[n] for n in COLS], axis=1)


class Steps:

    def __init__(self, eng, sem, per, base=0):
        self.eng, self.sem, self.per, self.base, self.n = eng, sem, per, base, 0

    def begin(self, turn):
        self.turn, self.n = turn, 0

    def did(self, ins):
        ins.then_inc(self.sem, 1)
        self.n += 1

    def settle(self):
        self.eng.wait_ge(self.sem, self.turn * self.per + self.base + self.n)

    def end(self):
        assert self.n == self.per, (self.sem, self.n)


def program(nc, a, out):
    ctx = ExitStack()
    with ctx:
        def sb(name, shape, dt=F32):
            return ctx.enter_context(nc.sbuf_tensor(name, shape, dt))

        def sem(name):
            return ctx.enter_context(nc.semaphore(name))

        PS = ctx.enter_context(nc.psum_tensor("PS", [P, 8, 512], F32))
        X = sb("X", [P, NT, D])
        CST = sb("CST", [P, NC_])

        def cst(name):
            o, w = COLS[name]
            return CST[:, o:o + w]

        ident = cst("ident")
        WQ, WK, WV = sb("WQ", [P, D]), sb("WK", [P, D]), sb("WV", [P, D])
        WP, WVP = sb("WP", [64, 2, D]), sb("WVP", [P, D])
        W1A, W2A = sb("W1A", [P, DA]), sb("W2A", [P, FA, D])
        COLA = sb("COLA", [P, 4])
        B1A = sb("B1A", [P, FA])
        ROWS = sb("ROWS", [1, 5, D])
        BVA = sb("BVA", [64, 2])
        WQB, WKB, WVB, WOB = (sb(n, [P, D]) for n in ("WQB", "WKB", "WVB", "WOB"))
        COLB = sb("COLB", [P, 3])
        WRN, WRT = sb("WRN", [NE, D]), sb("WRT", [P, NE])
        W1R, W2R = sb("W1R", [P, NE * KF, D]), sb("W2R", [P, NE, DFF])
        WA = sb("WA", [P, 2, NE, DFF], BF16)
        WB = sb("WB", [P, 2, NE, KF, D], BF16)
        ONES = sb("ONES", [1, P])
        WQK3 = sb("WQK3", [P, 2, NG, PIECES * 32])
        BQK3R = sb("BQK3R", [1, 2, NG, PIECES * 32])
        BQK3 = sb("BQK3", [P, 2, NG])
        I64B, WONEB = sb("I64B", [P, WIN], BF16), sb("WONEB", [P, P], BF16)
        BIASROW = sb("BIASROW", [1, 2, D])
        ST6, T3, MV = sb("ST6", [P, NT, 6]), sb("T3", [P, 4, NT]), sb("MV", [P, NT, 2])
        SM, VE, NHALF = sb("SM", [P, 4, NT]), sb("VE", [P, NT]), sb("NHALF", [P, NT])
        XN, XZ, HZ = (sb(n, [P, TB, D]) for n in ("XN", "XZ", "HZ"))
        XT = sb("XT", [P, SP_])
        QF = sb("QF", [P, 4, HALF])
        HI = sb("HI", [P, 2, HALF], BF16)
        QK = sb("QK", [P, 2, NG, SP_], BF16)
        QKM = sb("QKM", [P, 2, NG, 4, SP_], BF16)
        VB = sb("VB", [P, NU, 2, NPAIR, 2, 2, VW], BF16)
        NM = sb("NM", [P, 2, NH])
        R = sb("R", [P, 2, NH, WIN], BF16)
        PH, PL = sb("PH", [P, 2, NH * WIN], BF16), sb("PL", [P, 2, NH * WIN], BF16)
        PF = sb("PF", [P, 2, NH * WIN])
        DEN = sb("DEN", [P, 2, 2, NPAIR])
        C = sb("C", [P, 2, 2, NPAIR * HD])
        CTE, CTO = sb("CTE", [64, 2, SP_]), sb("CTO", [64, 2, SP_])
        RES2, HT = sb("RES2", [P, TB, D]), sb("HT", [P, S])
        H1 = sb("H1", [P, FA, S])
        FT = H1[:]
        FH, FL = (QKM[:, i].rearrange("p g h c -> p (g h c)")[:, 0:NT * P] for i in range(2))
        PR, PRE = sb("PR", [P, NT, NE]), sb("PRE", [P, NT, NE])
        GT, EQ = (PF[:, i, :].rearrange("p (j a c) -> p j a c", a=NE, c=NE) for i in range(2))
        RK, SE = sb("RK", [P, NT, NE]), sb("SE", [P, NT, NE])
        GS = sb("GS", [P, 4, NT])
        GATE = sb("GATE", [P, NT, NE])
        XR = W1R[:, 0:NT, :]
        HF = W1R[:].rearrange("p (c k a) d -> p c k (a d)", c=2, k=KF)
        HH, HL = (W2R[:, 4 * i:4 * i + 4, :].bitcast(BF16).rearrange("p (c a) (g s) -> p c (a g) s", c=2, s=S)
                  for i in range(2))
        XBT, QB, KB, OT = (H1[:, i, :] for i in range(4))
        VN, PN = (HT[:, 2 * D * i:2 * D * i + 2 * D].rearrange("p (c d) -> p c d", c=2) for i in range(2))
        BM, BS = sb("BM", [P, 2, 1]), sb("BS", [P, 2, 2])
        PT = RES2[:, 0:2, :]

        s = {n: sem(n) for n in (
            "ld_const", "ld_x", "ld_attn", "ld_moe", "ld_rows",
            "pool_consts", "ones_ready", "nhalf_ready", "bias_ps", "bias_ready",
            "wt_ps", "wt_hi", "wt_lo", "wr_ps", "wr_ready",
            "a_steps", "p_steps", "h_steps", "h_var", "h_rstd", "a_xz", "a_xt_ps", "a_xt", "a_qk_ps", "a_qf", "a_qk", "a_mask",
            "a_v_ps", "a_vh", "a_vl", "a_s", "a_nm", "a_r", "a_st", "a_ph", "a_pf", "a_pl",
            "a_o", "a_c", "a_ct_ps", "a_ct", "a_proj_ps", "a_pl_pool", "a_res2", "a_hz", "a_ht_ps",
            "a_ht", "a_h_ps", "a_h1", "a_y_ps", "a_x",
            "f_steps", "f_xz", "f_xt_ps", "f_fh", "f_ft", "f_fl", "f_lg_ps", "f_lg", "f_gate", "f_exp", "a_var", "a_rstd", "f_var", "f_rstd", "b_var", "b_rstd",
            "f_z", "f_hf", "f_hh", "f_hl", "f_y", "f_x",
            "b_steps", "b_xz", "b_xt_ps", "b_xt", "b_qk_ps", "b_qk", "b_s", "b_m", "b_p", "b_pn",
            "b_pt_ps", "b_pt", "b_v_ps", "b_v", "b_o", "b_oe", "b_ot", "b_y_ps", "b_x",
            "out_done")}

        ctx.enter_context(nc.allow_non_contiguous_dma(reason="small columns of biases"))
        block = ctx.enter_context(nc.Block())

        @block.sync
        def _(sp):
            def load(dst, src, name):
                sp.dma_start(dst, src).then_inc(s[name], 16)

            load(CST[:], a["cst"], "ld_const")
            xv = a["x"].rearrange("b (t p) d -> p (b t) d", p=P)
            load(X[:], xv, "ld_x")
            col = "(p o) -> p o"
            row = "(o d) -> o d"
            for i, n in enumerate(("bq", "bk", "bproj", "b2", "bo_b")):
                load(ROWS[:, i, :], a[n].rearrange(row, o=1), "ld_rows")
            load(BVA[:], a["bv"].rearrange("(h p) -> p h", h=2), "ld_rows")
            for i, n in enumerate(("ln1_g", "ln1_b", "ln2_g", "ln2_b")):
                load(COLA[:, i:i + 1], a[n].rearrange(col, o=1), "ld_rows")
            load(B1A[:], a["b1"].rearrange("(t p) -> p t", p=P), "ld_rows")
            for i, n in enumerate(("bq_b", "bk_b", "bv_b")):
                load(COLB[:, i:i + 1], a[n].rearrange(col, o=1), "ld_rows")
            load(WQ[:], a["wq"], "ld_attn")
            load(WK[:], a["wk"], "ld_attn")
            load(WV[:], a["wv"], "ld_attn")
            load(WP[:], a["wproj"].rearrange("(h p) n -> p h n", h=2), "ld_attn")
            load(W1A[:], a["w1"], "ld_attn")
            load(W2A[:], a["w2"].rearrange("(k p) n -> p k n", p=P), "ld_attn")
            for t, n in ((WQB, "Wq_b"), (WKB, "Wk_b"), (WVB, "Wv_b"), (WOB, "Wo_b")):
                load(t[:], a[n], "ld_attn")
            load(WRN[:], a["Wr"], "ld_moe")
            load(W1R[:], a["W1"].rearrange("e (k p) d -> p (e k) d", p=P), "ld_moe")
            load(W2R[:], a["W2"].rearrange("e d f -> d e f"), "ld_moe")
            sp.wait_ge(s["f_x"], 2 + 2 * NE * B)
            sp.dma_start(out.rearrange("b (t p) d -> p (b t) d", p=P), X[:]).then_inc(s["out_done"], 16)
            sp.wait_ge(s["out_done"], 16)

        LD_ROWS, LD_ATTN, LD_MOE = 16 * 14, 16 * 10, 16 * 3

        @block.gpsimd
        def _(pool):
            for name in PRIMED["gpsimd"]:
                pool.sem_inc(s[name], 1)
            nc.gpsimd.memset(NHALF[:], -0.5).then_inc(s["nhalf_ready"], 1)
            nc.gpsimd.memset(ONES[:], 1.0).then_inc(s["ones_ready"], 1)
            nc.gpsimd.memset(VB[:], 0.0).then_inc(s["pool_consts"], 1)
            nc.gpsimd.memset(QKM[:], 0.0).then_inc(s["pool_consts"], 1)
            nc.gpsimd.memset(CTE[:], 0.0).then_inc(s["pool_consts"], 1)
            nc.gpsimd.memset(CTO[:], 0.0).then_inc(s["pool_consts"], 1)
            pool.wait_ge(s["ld_const"], 16)
            nc.gpsimd.tensor_copy(I64B[:], cst("i64")).then_inc(s["pool_consts"], 1)
            nc.gpsimd.tensor_copy(WONEB[:], cst("wone")).then_inc(s["pool_consts"], 1)
            pool.wait_ge(s["ld_rows"], LD_ROWS)
            pool.wait_ge(s["ld_attn"], LD_ATTN)
            for m, w in enumerate((WQ, WK)):
                for hh in range(2):
                    for c in range(PIECES):
                        for src, dst in ((w[:, 64 * hh:64 * hh + 64], WQK3[:, m]),
                                         (ROWS[:, m, 64 * hh:64 * hh + 64], BQK3R[:, m])):
                            d = dst.rearrange("q g (pp h c d) -> q h c (g pp) d", pp=2, h=2, c=PIECES)
                            nc.gpsimd.tensor_copy(d[:, hh, c], src.rearrange("q (p d) -> q p d", d=HD)) \
                                .then_inc(s["pool_consts"], 1)
            nc.gpsimd.tensor_copy(WVP[:].rearrange("q (p h d) -> q h p d", h=2, d=HD),
                                  WV[:].rearrange("q (h p d) -> q h p d", h=2, d=HD)).then_inc(s["pool_consts"], 1)
            pool.wait_ge(s["pool_consts"], 1)
            for w in range(2):
                o = VB[:, :, 0, :, :, w, HD].rearrange("q u p h -> q u (p h)")
                v = cst("ones")[:, NU * w:NU * w + NU].unsqueeze(2).to_broadcast([P, NU, NH])
                nc.gpsimd.tensor_copy(o, v).then_inc(s["pool_consts"], 1)

            def unit_bias(turn, u):
                buf = u % 2
                pool.wait_ge(s["a_nm"], 1 + turn * 2 * NU + 2 * u + 2)
                if u >= 2:
                    pool.wait_ge(s["a_st"], 1 + turn * 2 * NU + 2 * (u - 1))
                else:
                    pool.wait_ge(s["a_st"], 1 + turn * 2 * NU)
                nc.gpsimd.tensor_tensor(
                    R[:, buf], NM[:, buf].unsqueeze(2).to_broadcast([P, NH, WIN]),
                    I64B[:].unsqueeze(1).to_broadcast([P, NH, WIN]), ALU.mult).then_inc(s["a_r"], 1)

            def rstd(k, name, n, c=TB, o=0):
                pool.wait_ge(s[name + "_var"], n)
                nc.gpsimd.tensor_tensor(SM[:, k, o:o + c], VE[:, o:o + c], NHALF[:, o:o + c], ALU.pow) \
                    .then_inc(s[name + "_rstd"], 1)

            def probabilities_lo(b, u):
                pool.wait_ge(s["a_pf"], 1 + b * 2 * NU + 2 * u + 2)
                half = slice(512, 1024)
                nc.gpsimd.tensor_tensor(PL[:, u % 2, half], PF[:, u % 2, half], PH[:, u % 2, half], ALU.subtract) \
                    .then_inc(s["a_pl_pool"], 1)

            def units(b):
                for t in range(NU + 1):
                    if t < NU:
                        unit_bias(b, t)
                    if t:
                        probabilities_lo(b, t - 1)

            pool.wait_ge(s["nhalf_ready"], 1)
            rstd(0, "a", 1)
            rstd(1, "a", 2)
            with pool.Fori(0, B - 1) as b:
                units(b)
                rstd(0, "a", b * 2 + 3)
                rstd(1, "a", b * 2 + 4)
                rstd(0, "h", b + 1, o=TB)
            units(B - 1)
            rstd(0, "h", B, o=TB)
            rstd(0, "f", 1, c=NT)
            with pool.Fori(0, B) as b:
                rstd(0, "b", b + 1)
            rstd(0, "f", 2, c=NT)

        XT_BANK = (4, 5, 6, 4)
        POOL_CONSTS = 7 + 2 * 2 * PIECES * 2 + 2
        NWT = 2 * NE

        @block.tensor
        def _(pe):
            mm = nc.tensor.matmul
            for name in PRIMED["tensor"]:
                pe.sem_inc(s[name], 1)

            def tr(dst, src, n=P):
                return nc.tensor.transpose(dst, src, ident[0:n, 0:n])

            pe.wait_ge(s["pool_consts"], POOL_CONSTS)
            pe.wait_ge(s["ones_ready"], 1)
            for m in range(2):
                for g in range(NG):
                    mm(PS[:, 7, m * NG + g:m * NG + g + 1], BQK3R[0:1, m, g, :], ONES[0:1, 0:1], start=True, stop=True)
            for hh in range(2):
                mm(PS[0:1, 6, 0:D], BVA[:, hh:hh + 1], WP[:, hh, :], start=hh == 0, stop=hh == 1)
            mm(PS[0:1, 6, D:2 * D], COLB[:, 2:3], WOB[:], start=True, stop=True).then_inc(s["bias_ps"], 1)
            pe.wait_ge(s["ld_moe"], LD_MOE)
            tr(PS[:, 5, 0:NE], WRN[:], NE).then_inc(s["wr_ps"], 1)
            for i in range(NWT):
                e, second = i // 2, i % 2
                if i >= 4:
                    pe.wait_ge(s["wt_lo"], i - 3)
                for k in range(KF):
                    src = W2R[:, e, k * P:k * P + P] if second else W1R[:, e * KF + k, :]
                    last = tr(PS[:, i % 4, k * P:k * P + P], src)
                last.then_inc(s["wt_ps"], 1)

            def x_t(b):
                pe.wait_ge(s["a_xz"], (b + 1) * TB)
                pe.wait_ge(s["a_c"], 1 + b * 2 * NU)
                for j in range(TB):
                    last = tr(PS[:, 5, j * P:j * P + P], XZ[:, j, :])
                last.then_inc(s["a_xt_ps"], 1)

            def project_qk(b, blocks):
                for n in blocks:
                    if n == 0:
                        pe.wait_ge(s["a_xt"], (b + 1) * 3)
                    if n >= 2:
                        pe.wait_ge(s["a_qf"], b * 16 + n - 1)
                    m, g, h = n // 8, n // 2 % 4, n % 2
                    mm(PS[:, 4 + n % 2, 0:HALF], WQK3[:, m, g, :], XT[:, h * HALF:(h + 1) * HALF],
                       start=True, stop=True).then_inc(s["a_qk_ps"], 1)

            def units(b):
                def scores(u):
                    for k in range(2):
                        pe.wait_ge(s["a_nm"], 1 + b * 2 * NU + max(0, 2 * u + k - 1) if u else b * 2 * NU)
                        for g in (2 * k, 2 * k + 1):
                            for w in range(2):
                                c = C0[u] + WIN * w
                                o = PS[64 * w:64 * w + 64, k, (g % 2) * 256:(g % 2) * 256 + 256]
                                last = mm(o, QK[:, 0, g, c:c + WIN], QKM[:, 1, g, :, c:c + WIN],
                                          start=g % 2 == 0, stop=g % 2 == 1, skip_group_check=True)
                        last.then_inc(s["a_s"], 1)

                def values(u):
                    if u == 0:
                        pe.wait_ge(s["a_res2"], 1 + b)
                    else:
                        pe.wait_ge(s["a_vl"], b * 2 * NU + 2 * u)
                    mm(PS[:, 6, 0:D], XT[:, C0[u]:C0[u] + P], WVP[:], start=True, stop=True) \
                        .then_inc(s["a_v_ps"], 1)

                def scores_t(u):
                    pe.wait_ge(s["a_r"], 1 + b * NU + u + 1)
                    for k in range(2):
                        pe.wait_ge(s["a_pf"], 1 + b * 2 * NU + (2 * (u - 1) + k + 1 if u else 0))
                        mm(PS[:, 2 + k, :], WONEB[:], R[:, u % 2, 8 * k:8 * k + 8, :], start=True, stop=False,
                           skip_group_check=True)
                        for g in (2 * k, 2 * k + 1):
                            for w in range(2):
                                c = C0[u] + WIN * w
                                o = PS[64 * w:64 * w + 64, 2 + k, (g % 2) * 256:(g % 2) * 256 + 256]
                                last = mm(o, QK[:, 1, g, c:c + WIN], QKM[:, 0, g, :, c:c + WIN],
                                          start=False, stop=True, skip_group_check=True)
                        last.then_inc(s["a_st"], 1)

                def weighted(u):
                    buf = u % 2
                    pe.wait_ge(s["a_pl"], b * NU + u + 1)
                    pe.wait_ge(s["a_pl_pool"], b * NU + u + 1)
                    pe.wait_ge(s["a_vl"], b * 2 * NU + 2 * u + 2)
                    pe.wait_ge(s["a_c"], 1 + b * 2 * NU + (2 * (u - 1) if u >= 2 else 0))
                    n = 4 * VW
                    for p in range(NPAIR):
                        o = PS[:, 4 + buf, n * p:n * p + n]
                        vh = VB[:, u, 0, p].rearrange("q h w v -> q (h w v)")
                        vl = VB[:, u, 1, p].rearrange("q h w v -> q (h w v)")
                        mm(o, PH[:, buf, P * p:P * p + P], vh, start=True, stop=False)
                        mm(o, PH[:, buf, P * p:P * p + P], vl, start=False, stop=False)
                        last = mm(o, PL[:, buf, P * p:P * p + P], vh, start=False, stop=True)
                    last.then_inc(s["a_o"], 1)

                def context_t(u):
                    pe.wait_ge(s["a_c"], 1 + b * 2 * NU + 2 * (u + 1))
                    pe.wait_ge(s["a_ct"], 1 + b * 2 * NU + 2 * u)
                    tr(PS[:, 7, 0:P], C[:, u % 2].rearrange("q w c -> q (w c)")).then_inc(s["a_ct_ps"], 1)

                pe.wait_ge(s["a_mask"], (b + 1) * 8)
                for t in range(NU + 3):
                    if t < NU:
                        scores(t)
                        values(t)
                    if 1 <= t <= NU:
                        scores_t(t - 1)
                    if 2 <= t <= NU + 1:
                        weighted(t - 2)
                    if 3 <= t:
                        context_t(t - 3)

            def project(b):
                pe.wait_ge(s["a_ct"], 1 + (b + 1) * 2 * NU)
                for j in range(TB):
                    o = PS[:, 6, j * D:j * D + D]
                    mm(o, ONES[:], BIASROW[:, 0, :], start=True, stop=False)
                    for hh in range(2):
                        for ct in (CTE, CTO):
                            last = mm(o, ct[:, hh, PAD + j * P:PAD + j * P + P], WP[:, hh, :], start=False,
                                      stop=hh == 1 and ct is CTO)
                last.then_inc(s["a_proj_ps"], 1)

            def h_t(b):
                pe.wait_ge(s["a_hz"], (b + 1) * TB)
                for j in range(TB):
                    last = tr(PS[:, 7, j * P:j * P + P], HZ[:, j, :])
                last.then_inc(s["a_ht_ps"], 1)

            def hidden_a(b, f):
                if f == 0:
                    pe.wait_ge(s["a_ht"], b + 1)
                mm(PS[:, f, :], W1A[:, f * P:f * P + P], HT[:], start=True, stop=True).then_inc(s["a_h_ps"], 1)

            def output_a(b):
                pe.wait_ge(s["a_h1"], (b + 1) * FA)
                for j in range(TB):
                    o = PS[:, 6, j * D:j * D + D]
                    mm(o, ONES[:], ROWS[:, 3, :], start=True, stop=False)
                    for k in range(FA):
                        last = mm(o, H1[:, k, j * P:j * P + P], W2A[:, k, :], start=False, stop=k == FA - 1)
                last.then_inc(s["a_y_ps"], 1)

            pe.wait_ge(s["bias_ready"], 4)
            pe.wait_ge(s["wr_ready"], 1)
            x_t(0)
            project_qk(0, range(16))
            with pe.Fori(0, B - 1) as b:
                units(b)
                project(b)
                x_t(b + 1)
                h_t(b)
                for f in range(FA):
                    project_qk(b + 1, range(4 * f, 4 * f + 4))
                    hidden_a(b, f)
                output_a(b)
            units(B - 1)
            project(B - 1)
            h_t(B - 1)
            for f in range(FA):
                hidden_a(B - 1, f)
            output_a(B - 1)

            def experts(f):
                for c in range(B):
                    pe.wait_ge(s["f_xz"], f * NT + (c + 1) * TB)
                    if c == 3:
                        pe.wait_ge(s["f_fl"], f * B + 1)
                    for j in range(TB):
                        last = tr(PS[:, XT_BANK[c], j * P:j * P + P], XR[:, c * TB + j, :])
                    last.then_inc(s["f_xt_ps"], 1)
                for c in range(B):
                    pe.wait_ge(s["f_ft"], f * B + c + 1)
                    for j in range(TB):
                        t = c * TB + j
                        last = mm(PS[:, 7, t * NE:t * NE + NE], FT[:, c, j * P:j * P + P], WRT[:], start=True, stop=True)
                last.then_inc(s["f_lg_ps"], 1)
                pe.wait_ge(s["f_fl"], (f + 1) * B)

                def hidden(e, c):
                    i = f * NE * B + e * B + c
                    for k in range(KF):
                        if isinstance(e, int) and e == 0 and c == 0:
                            pe.wait_ge(s["f_hh"], 1 + f * NE * B * KF)
                        else:
                            pe.wait_ge(s["f_hh"], 1 + i * KF - KF + k + 1)
                        o = PS[:, k, :]
                        wh, wl = WA[:, 0, e, k * P:k * P + P], WA[:, 1, e, k * P:k * P + P]
                        xh, xl = FH[:, c * S:c * S + S], FL[:, c * S:c * S + S]
                        mm(o, wh, xh, start=True, stop=False)
                        mm(o, wh, xl, start=False, stop=False)
                        mm(o, wl, xh, start=False, stop=True).then_inc(s["f_z"], 1)

                def outputs(e, c):
                    i = f * NE * B + e * B + c
                    pe.wait_ge(s["f_hl"], (i + 1) * KF)
                    pe.wait_ge(s["f_x"], i + 1)
                    for j in range(TB):
                        o = PS[:, 4 + c % 2, j * D:j * D + D]
                        for k in range(KF):
                            hh, hl = HH[:, c % 2, k, j * P:j * P + P], HL[:, c % 2, k, j * P:j * P + P]
                            mm(o, hh, WB[:, 0, e, k, :], start=k == 0, stop=False)
                            mm(o, hh, WB[:, 1, e, k, :], start=False, stop=False)
                            last = mm(o, hl, WB[:, 0, e, k, :], start=False, stop=k == KF - 1)
                    last.then_inc(s["f_y"], 1)

                hidden(0, 0)
                with pe.Fori(0, NE - 1) as e:
                    for c in range(B):
                        hidden(e if c < B - 1 else e + 1, (c + 1) % B)
                        outputs(e, c)
                for c in range(B):
                    if c < B - 1:
                        hidden(NE - 1, c + 1)
                    outputs(NE - 1, c)

            pe.wait_ge(s["a_x"], B)
            experts(0)

            def attention_b(b):
                pe.wait_ge(s["b_xz"], (b + 1) * TB)
                for j in range(TB):
                    last = tr(PS[:, 6, j * P:j * P + P], XZ[:, j, :])
                last.then_inc(s["b_xt_ps"], 1)
                pe.wait_ge(s["b_xt"], b + 1)
                pe.wait_ge(s["b_x"], 1 + b)
                mm(PS[:, 7, :], WQB[:], XBT, start=True, stop=True).then_inc(s["b_qk_ps"], 1)
                mm(PS[:, 0, :], WKB[:], XBT, start=True, stop=True).then_inc(s["b_qk_ps"], 1)
                pe.wait_ge(s["b_qk"], (b + 1) * 2)

                def scores(w):
                    c = w * P // 2
                    pe.wait_ge(s["b_p"], 1 + b * NW + (w - 1 if w >= 2 else 0))
                    mm(PS[:, 1 + w % 2, 0:P], QB[:, c:c + P], KB[:, c:c + P], start=True, stop=True) \
                        .then_inc(s["b_s"], 1)
                    pe.wait_ge(s["b_v"], 1 + b * NW + w)
                    mm(PS[:, 3, 0:D], XBT[:, c:c + P], WVB[:], start=True, stop=True).then_inc(s["b_v_ps"], 1)

                def weighted(w):
                    pe.wait_ge(s["b_pn"], b * NW + w + 1)
                    pe.wait_ge(s["b_pt"], 1 + b * NW + w)
                    tr(PS[:, 4, 0:P], PN[:, w % 2, :]).then_inc(s["b_pt_ps"], 1)
                    pe.wait_ge(s["b_pt"], 1 + b * NW + w + 1)
                    pe.wait_ge(s["b_v"], 1 + b * NW + w + 1)
                    c = w // 2 * P
                    mm(PS[:, 0 if w % 2 else 5, c:c + P], VN[:, w % 2, :], PT[:, w % 2, :], start=True, stop=True) \
                        .then_inc(s["b_o"], 1)

                for t in range(NW + 1):
                    if t < NW:
                        scores(t)
                    if t:
                        weighted(t - 1)
                pe.wait_ge(s["b_ot"], b + 1)
                for j in range(TB):
                    o = PS[:, 7, j * D:j * D + D]
                    mm(o, ONES[:], BIASROW[:, 1, :], start=True, stop=False)
                    last = mm(o, OT[:, j * P:j * P + P], WOB[:], start=False, stop=True)
                last.then_inc(s["b_y_ps"], 1)

            pe.wait_ge(s["f_x"], 2 + NE * B)
            with pe.Fori(0, B) as b:
                attention_b(b)
            pe.wait_ge(s["b_x"], 1 + B)
            experts(1)

        @block.scalar
        def _(act):
            fn = nc.scalar.activation
            for name in PRIMED["scalar"]:
                act.sem_inc(s[name], 1)
            act.wait_ge(s["bias_ps"], 1)
            fn(BQK3[:, 0, :], PS[:, 7, 0:NG], ACT.Copy, scale=SCALE_A).then_inc(s["bias_ready"], 1)
            fn(BQK3[:, 1, :], PS[:, 7, NG:2 * NG], ACT.Copy).then_inc(s["bias_ready"], 1)
            act.wait_ge(s["wr_ps"], 1)
            fn(WRT[:], PS[:, 5, 0:NE], ACT.Copy).then_inc(s["wr_ready"], 1)
            for i in range(NWT):
                e, second = i // 2, i % 2
                act.wait_ge(s["wt_ps"], i + 1)
                o = WB[:, 0, e].rearrange("p k d -> p (k d)") if second else WA[:, 0, e, :]
                fn(o, PS[:, i % 4, :], ACT.Copy).then_inc(s["wt_hi"], 1)

            def x_t(b):
                act.wait_ge(s["a_xt_ps"], b + 1)
                for dst, src, w in ((PAD, 0, S), (0, 0, PAD), (PAD + S, S - PAD, PAD)):
                    fn(XT[:, dst:dst + w], PS[:, 5, src:src + w], ACT.Identity, scale=COLA[:, 0:1],
                       bias=COLA[:, 1:2]).then_inc(s["a_xt"], 1)

            def qk_out(b, blocks):
                for n in blocks:
                    m, g = n // 8, n // 2 % 4
                    act.wait_ge(s["a_qk_ps"], b * 16 + n + 1)
                    act.wait_ge(s["a_qk"], 1 + b * 16 + (n - 3 if n >= 4 else 0))
                    fn(QF[:, n % 4, :], PS[:, 4 + n % 2, 0:HALF], ACT.Identity,
                       scale=SCALE_A if m == 0 else 1.0, bias=BQK3[:, m, g:g + 1]).then_inc(s["a_qf"], 1)

            def units(b):
                def values_hi(u):
                    act.wait_ge(s["a_v_ps"], b * NU + u + 1)
                    for w in range(2):
                        rows = slice(64 * w, 64 * w + 64)
                        fn(VB[rows, u, 0, :, :, w, 0:HD].rearrange("q p h d -> q (p h) d"),
                           PS[rows, 6, 0:D].rearrange("q (c d) -> q c d", d=HD), ACT.Copy,
                           scale=cst("valid")[rows, u:u + 1]).then_inc(s["a_vh"], 1)

                def exponentials(u):
                    buf = u % 2
                    act.wait_ge(s["a_o"], 1 + b * NU + (u - 1 if u >= 2 else 0))
                    for k in range(2):
                        act.wait_ge(s["a_st"], 1 + b * 2 * NU + 2 * u + k + 1)
                        half = slice(512 * k, 512 * k + 512)
                        fn(PH[:, buf, half], PS[:, 2 + k, :], ACT.Exp).then_inc(s["a_ph"], 1)
                        fn(PF[:, buf, half], PS[:, 2 + k, :], ACT.Exp).then_inc(s["a_pf"], 1)

                def context_out(u):
                    k, odd = UNITS[u]
                    act.wait_ge(s["a_ct_ps"], 1 + b * NU + u + 1)
                    for w in range(2):
                        c = C0[u] + WIN * w
                        fn((CTO if odd else CTE)[:, :, c:c + WIN],
                           PS[64 * w:64 * w + 64, 7, 0:P].rearrange("c (h q) -> c h q", h=2), ACT.Copy) \
                            .then_inc(s["a_ct"], 1)

                act.wait_ge(s["a_proj_ps"], 1 + b)
                for t in range(NU + 3):
                    if t < NU:
                        values_hi(t)
                    if 1 <= t <= NU:
                        exponentials(t - 1)
                    if 3 <= t:
                        context_out(t - 3)

            def h_t(b):
                act.wait_ge(s["a_ht_ps"], b + 1)
                fn(HT[:], PS[:, 7, :], ACT.Identity, scale=COLA[:, 2:3], bias=COLA[:, 3:4]).then_inc(s["a_ht"], 1)

            def gelu(b, k):
                act.wait_ge(s["a_h_ps"], b * FA + k + 1)
                fn(H1[:, k, :], PS[:, k, :], ACT.Gelu, bias=B1A[:, k:k + 1]).then_inc(s["a_h1"], 1)

            act.wait_ge(s["ld_rows"], LD_ROWS)
            x_t(0)
            qk_out(0, range(16))
            with act.Fori(0, B - 1) as b:
                units(b)
                x_t(b + 1)
                h_t(b)
                for k in range(FA):
                    qk_out(b + 1, range(4 * k, 4 * k + 4))
                    gelu(b, k)
            units(B - 1)
            h_t(B - 1)
            for k in range(FA):
                gelu(B - 1, k)

            def experts(f):
                for c in range(B):
                    act.wait_ge(s["f_xt_ps"], f * B + c + 1)
                    fn(FH[:, c * S:c * S + S], PS[:, XT_BANK[c], :], ACT.Copy).then_inc(s["f_fh"], 1)
                    fn(FT[:, c, :], PS[:, XT_BANK[c], :], ACT.Copy).then_inc(s["f_ft"], 1)

                def silu(e, c):
                    i = f * NE * B + e * B + c
                    for k in range(KF):
                        act.wait_ge(s["f_z"], i * KF + k + 1)
                        if isinstance(e, int) and e == 0 and c < 2:
                            act.wait_ge(s["f_y"], f * NE * B)
                        else:
                            act.wait_ge(s["f_y"], i - 1)
                        fn(HF[:, c % 2, k, :], PS[:, k, :], ACT.Silu).then_inc(s["f_hf"], 1)
                        fn(HH[:, c % 2, k, :], PS[:, k, :], ACT.Silu).then_inc(s["f_hh"], 1)

                silu(0, 0)
                act.wait_ge(s["f_lg"], f + 1)
                fn(PRE[:], PR[:], ACT.Exp).then_inc(s["f_exp"], 1)
                silu(0, 1)
                with act.Fori(0, NE - 1) as e:
                    for c in range(B):
                        silu(e if c < B - 2 else e + 1, (c + 2) % B)
                for c in range(2):
                    silu(NE - 1, c + 2)

            experts(0)

            def attention_b(b):
                act.wait_ge(s["b_xt_ps"], b + 1)
                act.wait_ge(s["b_v_ps"], 1 + b * NW)
                fn(XBT, PS[:, 6, :], ACT.Copy).then_inc(s["b_xt"], 1)
                for m, (dst, bank) in enumerate(((QB, 7), (KB, 0))):
                    act.wait_ge(s["b_qk_ps"], b * 2 + m + 1)
                    fn(dst, PS[:, bank, :], ACT.Identity, bias=COLB[:, m:m + 1]).then_inc(s["b_qk"], 1)

                def softmax(w):
                    act.wait_ge(s["b_v_ps"], 1 + b * NW + w + 1)
                    act.wait_ge(s["b_o"], 1 + b * NW + (w - 1 if w >= 2 else 0))
                    fn(VN[:, w % 2, :], PS[:, 3, 0:D], ACT.Copy).then_inc(s["b_v"], 1)
                    act.wait_ge(s["b_m"], b * NW + w + 1)
                    act.wait_ge(s["b_pt_ps"], 1 + b * NW + (w - 1 if w >= 2 else 0))
                    fn(PN[:, w % 2, :], PS[:, 1 + w % 2, 0:P], ACT.Exp, scale=SCALE_B, bias=BM[:, w % 2, :],
                       accum_out=BS[:, w % 2, 0:1]).then_inc(s["b_p"], 1)

                def transposed(w):
                    act.wait_ge(s["b_pt_ps"], 1 + b * NW + w + 1)
                    fn(PT[:, w % 2, :], PS[:, 4, 0:P], ACT.Copy).then_inc(s["b_pt"], 1)

                for t in range(NW + 1):
                    if t < NW:
                        softmax(t)
                    if t:
                        transposed(t - 1)

            with act.Fori(0, B) as b:
                attention_b(b)
            experts(1)

        @block.vector
        def _(dve):
            v = nc.vector
            for name in PRIMED["vector"]:
                dve.sem_inc(s[name], 1)
            dve.sem_inc(s["f_x"], 2)
            dve.wait_ge(s["bias_ps"], 1)
            dve.wait_ge(s["bias_ready"], 2)
            for i, r in enumerate((2, 4)):
                v.tensor_tensor(BIASROW[:, i, :], PS[0:1, 6, D * i:D * i + D], ROWS[:, r, :], ALU.add) \
                    .then_inc(s["bias_ready"], 1)
            for i in range(NWT):
                e, second = i // 2, i % 2
                dve.wait_ge(s["wt_hi"], i + 1)
                hi = WB[:, 0, e].rearrange("p k d -> p (k d)") if second else WA[:, 0, e, :]
                lo = WB[:, 1, e].rearrange("p k d -> p (k d)") if second else WA[:, 1, e, :]
                v.tensor_tensor(lo, PS[:, i % 4, :], hi, ALU.subtract).then_inc(s["wt_lo"], 1)
            dve.wait_ge(s["ld_x"], 16)

            def variance(st, tile, var, c=TB, o=0):
                at = slice(o, o + c)
                for j in range(c):
                    st.did(v.bn_stats(ST6[:, o + j, :], tile(j)))
                st.settle()
                st.did(v.tensor_tensor(T3[:, 0, at], ST6[:, at, 1], ST6[:, at, 4], ALU.add))
                st.did(v.tensor_tensor(T3[:, 1, at], ST6[:, at, 1], ST6[:, at, 4], ALU.subtract))
                st.did(v.tensor_tensor(T3[:, 2, at], ST6[:, at, 2], ST6[:, at, 5], ALU.add))
                st.settle()
                st.did(v.tensor_scalar(MV[:, at, 0], T3[:, 0, at], 0.5, None, ALU.mult))
                st.did(v.scalar_tensor_tensor(T3[:, 3, at], T3[:, 1, at], 0.25, T3[:, 1, at], ALU.mult, ALU.mult))
                st.settle()
                st.did(v.scalar_tensor_tensor(MV[:, at, 1], T3[:, 2, at], 1.0 / D, T3[:, 3, at], ALU.mult, ALU.add))
                st.settle()
                v.tensor_scalar(VE[:, at], MV[:, at, 1], EPS, None, ALU.add).then_inc(s[var], 1)

            def stats(st, tile, var, n, c=TB):
                variance(st, tile, var, c)
                dve.wait_ge(s[var.replace("var", "rstd")], n)

            def normalise(dst, tile, r, name, c=TB, o=0):
                for j in range(c):
                    v.tensor_scalar(dst[:, j, :], tile(j), MV[:, o + j, 0:1], SM[:, r, o + j:o + j + 1],
                                    ALU.subtract, ALU.mult).then_inc(s[name], 1)

            ps = Steps(dve, s["p_steps"], TB + 6 + 3 + TB + 16)
            st = Steps(dve, s["a_steps"], 3 * NU)
            hs = Steps(dve, s["h_steps"], 1 + TB + 6)

            def input_variance(b):
                ps.begin(b)
                variance(ps, lambda j: X[:, TB * b + j, :], "a_var")
                dve.wait_ge(s["a_rstd"], b * 2 + 1)
                ps.did(v.tensor_tensor(SM[:, 1, 0:TB], MV[:, 0:TB, 1], SM[:, 0, 0:TB], ALU.mult))
                ps.settle()
                ps.did(v.tensor_tensor(SM[:, 2, 0:TB], SM[:, 1, 0:TB], SM[:, 0, 0:TB], ALU.mult))
                ps.settle()
                v.tensor_scalar(VE[:, 0:TB], SM[:, 2, 0:TB], EPS, None, ALU.add).then_inc(s["a_var"], 1)

            def input_normalised(b):
                x_tile = lambda j: X[:, TB * b + j, :]
                dve.wait_ge(s["a_rstd"], b * 2 + 2)
                ps.did(v.tensor_tensor(SM[:, 3, 0:TB], SM[:, 1, 0:TB], SM[:, 0, 0:TB], ALU.mult))
                ps.settle()
                normalise(XZ, x_tile, 3, "a_xz")
                for j in range(TB):
                    ps.did(v.tensor_scalar(XN[:, j, :], x_tile(j), MV[:, j, 0:1], SM[:, 0, j:j + 1],
                                           ALU.subtract, ALU.mult))

            def split_qk(b, m):
                for n in range(8 * m, 8 * m + 8):
                    g, h = n // 2 % 4, n % 2
                    cols = slice(h * HALF, (h + 1) * HALF)
                    dve.wait_ge(s["a_qf"], b * 16 + n + 1)
                    ps.did(v.tensor_copy(HI[:, n % 2, :], QF[:, n % 4, :]))
                    ps.settle()
                    v.scalar_tensor_tensor(QK[:, m, g, cols], HI[:, n % 2, :], cst("mk" if m else "mq"),
                                           QF[:, n % 4, :], ALU.mult, ALU.add).then_inc(s["a_qk"], 1)
                dve.wait_ge(s["a_qk"], 1 + b * 16 + 8 * (m + 1))
                for i in range(4):
                    rows = slice(32 * i, 32 * i + 32)
                    v.tensor_copy(QKM[rows, m, :, i, :], QK[rows, m, :, :]).then_inc(s["a_mask"], 1)

            def units(b):
                st.begin(b)

                def maxima(u):
                    for k in range(2):
                        dve.wait_ge(s["a_s"], b * 2 * NU + 2 * u + k + 1)
                        dve.wait_ge(s["a_r"], 1 + b * NU + (u - 1 if u >= 2 else 0))
                        v.tensor_reduce(NM[:, u % 2, 8 * k:8 * k + 8],
                                        PS[:, k, :].rearrange("q (h c) -> q h c", c=WIN), op=ALU.max, axis=AXX,
                                        negate=True).then_inc(s["a_nm"], 1)

                def values_lo(u):
                    dve.wait_ge(s["a_vh"], b * 2 * NU + 2 * u + 2)
                    for w in range(2):
                        rows = slice(64 * w, 64 * w + 64)
                        hi, lo = (VB[rows, u, i, :, :, w, 0:HD].rearrange("q p h d -> q (p h) d") for i in range(2))
                        v.scalar_tensor_tensor(lo, PS[rows, 6, 0:D].rearrange("q (c d) -> q c d", d=HD),
                                               cst("valid")[rows, u:u + 1], hi, ALU.mult, ALU.subtract) \
                            .then_inc(s["a_vl"], 1)

                def probabilities_lo(u):
                    half = slice(0, 512)
                    dve.wait_ge(s["a_pf"], 1 + b * 2 * NU + 2 * u + 1)
                    v.tensor_tensor(PL[:, u % 2, half], PF[:, u % 2, half], PH[:, u % 2, half], ALU.subtract) \
                        .then_inc(s["a_pl"], 1)

                def normalised(u):
                    buf = u % 2
                    dve.wait_ge(s["a_o"], 1 + b * NU + u + 1)
                    dve.wait_ge(s["a_ct_ps"], 1 + b * NU + (u - 1 if u >= 2 else 0))

                    def o(hh):
                        return PS[64 * hh:64 * hh + 64, 4 + buf, 0:4 * VW * NPAIR].rearrange(
                            "q (p h w v) -> q h w p v", p=NPAIR, h=2, w=2)[:, hh]
                    for hh in range(2):
                        rows = slice(64 * hh, 64 * hh + 64)
                        st.did(v.reciprocal(DEN[rows, buf], o(hh)[:, :, :, HD]))
                    st.settle()
                    bl = cst("blend")[:, 2 * u:2 * u + 2].unsqueeze(2).to_broadcast([P, 2, NPAIR])
                    st.did(v.tensor_tensor(DEN[:, buf], DEN[:, buf], bl, ALU.mult))
                    st.settle()
                    for hh in range(2):
                        rows = slice(64 * hh, 64 * hh + 64)
                        d = DEN[rows, buf].unsqueeze(3).to_broadcast([64, 2, NPAIR, HD])
                        v.tensor_tensor(C[rows, buf].rearrange("q w (p d) -> q w p d", d=HD),
                                        o(hh)[:, :, :, 0:HD], d, ALU.mult).then_inc(s["a_c"], 1)

                for t in range(NU + 2):
                    if t < NU:
                        maxima(t)
                        values_lo(t)
                    if 1 <= t <= NU:
                        probabilities_lo(t - 1)
                    if 2 <= t:
                        normalised(t - 2)
                st.end()

            res = lambda j: RES2[:, j, :]

            def residual(b):
                dve.wait_ge(s["a_proj_ps"], 1 + b + 1)
                hs.begin(b)
                hs.did(v.tensor_tensor(RES2[:], PS[:, 6, :].rearrange("p (j d) -> p j d", d=D), XN[:], ALU.add))
                hs.settle()
                variance(hs, res, "h_var", o=TB)
                hs.end()

            def residual_normalised(b):
                dve.wait_ge(s["h_rstd"], b + 1)
                normalise(HZ, res, 0, "a_hz", o=TB)

            def output_a(b):
                dve.wait_ge(s["a_y_ps"], b + 1)
                xs = X[:, bass.ds(TB * b, TB), :]
                v.tensor_tensor(RES2[:], PS[:, 6, :].rearrange("p (j d) -> p j d", d=D), RES2[:], ALU.add) \
                    .then_inc(s["a_res2"], 1)
                dve.wait_ge(s["a_res2"], 1 + b + 1)
                v.tensor_tensor(xs, xs, RES2[:], ALU.add).then_inc(s["a_x"], 1)

            input_variance(0)
            input_normalised(0)
            for m in range(2):
                split_qk(0, m)
            ps.end()
            with dve.Fori(0, B - 1) as b:
                units(b)
                input_variance(b + 1)
                residual(b)
                input_normalised(b + 1)
                residual_normalised(b)
                for m in range(2):
                    split_qk(b + 1, m)
                ps.end()
                output_a(b)
            units(B - 1)
            residual(B - 1)
            residual_normalised(B - 1)
            output_a(B - 1)
            dve.wait_ge(s["a_x"], B)

            F_STEPS = NT + 6 + 9

            def experts(f):
                fs = Steps(dve, s["f_steps"], F_STEPS)

                fs.begin(f)
                x_tile = lambda j: X[:, j, :]
                stats(fs, x_tile, "f_var", f + 1, NT)
                normalise(XR, x_tile, 0, "f_xz", NT)
                for c in range(B):
                    dve.wait_ge(s["f_ft"], f * B + c + 1)
                    cols = slice(S * c, S * c + S)
                    v.tensor_tensor(FL[:, cols], PS[:, XT_BANK[c], :], FH[:, cols], ALU.subtract).then_inc(s["f_fl"], 1)

                def gates():
                    dve.wait_ge(s["f_lg_ps"], f + 1)
                    lg = PS[:, 7, 0:NT * NE].rearrange("p (j e) -> p j e", e=NE)
                    fs.did(v.tensor_reduce(GS[:, 0, :], lg, op=ALU.max, axis=AXX))
                    fs.settle()
                    v.tensor_tensor(PR[:], lg, GS[:, 0, :].unsqueeze(2).to_broadcast([P, NT, NE]), ALU.subtract) \
                        .then_inc(s["f_lg"], 1)
                    dve.wait_ge(s["f_lg"], f + 1)
                    own = PR[:].unsqueeze(3).to_broadcast([P, NT, NE, NE])
                    other = PR[:].unsqueeze(2).to_broadcast([P, NT, NE, NE])
                    fs.did(v.tensor_tensor(EQ, other, own, ALU.is_equal))
                    fs.did(v.tensor_tensor(GT, other, own, ALU.is_gt))
                    fs.settle()
                    low = cst("lower").unsqueeze(1).to_broadcast([P, NT, NE * NE])
                    flat = EQ.rearrange("p j a c -> p j (a c)")
                    fs.did(v.tensor_tensor(flat, flat, low, ALU.mult))
                    fs.settle()
                    fs.did(v.tensor_tensor(GT, GT, EQ, ALU.add))
                    fs.settle()
                    fs.did(v.tensor_reduce(RK[:], GT, op=ALU.add, axis=AXX))
                    fs.settle()
                    dve.wait_ge(s["f_exp"], f + 1)
                    fs.did(v.scalar_tensor_tensor(SE[:], RK[:], 1.5, PRE[:], ALU.is_lt, ALU.mult))
                    fs.settle()
                    fs.did(v.tensor_reduce(GS[:, 1, :], SE[:], op=ALU.add, axis=AXX))
                    fs.settle()
                    fs.did(v.reciprocal(GS[:, 2, :], GS[:, 1, :]))
                    fs.settle()
                    v.tensor_tensor(GATE[:], SE[:], GS[:, 2, :].unsqueeze(2).to_broadcast([P, NT, NE]), ALU.mult) \
                        .then_inc(s["f_gate"], 1)
                    fs.end()

                def hidden_lo(e, c):
                    i = f * NE * B + e * B + c
                    for k in range(KF):
                        dve.wait_ge(s["f_hh"], 1 + i * KF + k + 1)
                        v.tensor_tensor(HL[:, c % 2, k, :], HF[:, c % 2, k, :], HH[:, c % 2, k, :], ALU.subtract) \
                            .then_inc(s["f_hl"], 1)

                def combine(e, c):
                    i = f * NE * B + e * B + c
                    dve.wait_ge(s["f_y"], i + 1)
                    for j in range(TB):
                        t = c * TB + j
                        last = v.scalar_tensor_tensor(X[:, t, :], PS[:, 4 + c % 2, j * D:j * D + D], GATE[:, t, gate_col(e)],
                                                      X[:, t, :], ALU.mult, ALU.add)
                    last.then_inc(s["f_x"], 1)

                def gate_col(e):
                    return bass.ds(e, 1)

                hidden_lo(0, 0)
                gates()
                dve.wait_ge(s["f_gate"], f + 1)
                with dve.Fori(0, NE - 1) as e:
                    for c in range(B):
                        hidden_lo(e if c < B - 1 else e + 1, (c + 1) % B)
                        combine(e, c)
                for c in range(B):
                    if c < B - 1:
                        hidden_lo(NE - 1, c + 1)
                    combine(NE - 1, c)
                dve.wait_ge(s["f_x"], 2 + NE * B * (f + 1))

            experts(0)

            B_STEPS = TB + 6 + 2 * NW + 1
            bs = Steps(dve, s["b_steps"], B_STEPS)

            def attention_b(b):
                bs.begin(b)
                x_tile = lambda j: X[:, TB * b + j, :]
                stats(bs, x_tile, "b_var", b + 1)
                normalise(XZ, x_tile, 0, "b_xz")

                def row_max(w):
                    dve.wait_ge(s["b_s"], b * NW + w + 1)
                    dve.wait_ge(s["b_p"], 1 + b * NW + (w - 1 if w >= 2 else 0))
                    bs.did(v.tensor_reduce(BM[:, w % 2, :], PS[:, 1 + w % 2, 0:P], op=ALU.max, axis=AXX, negate=True))
                    bs.settle()
                    v.tensor_scalar(BM[:, w % 2, :], BM[:, w % 2, :], SCALE_B, None, ALU.mult).then_inc(s["b_m"], 1)

                def divide(w):
                    dve.wait_ge(s["b_p"], 1 + b * NW + w + 1)
                    bs.did(v.reciprocal(BS[:, w % 2, 1:2], BS[:, w % 2, 0:1]))
                    bs.settle()
                    v.tensor_scalar(PN[:, w % 2, :], PN[:, w % 2, :], BS[:, w % 2, 1:2], cst("cnt")[:, w:w + 1],
                                    ALU.mult, ALU.mult).then_inc(s["b_pn"], 1)

                for t in range(NW + 1):
                    if t < NW:
                        row_max(t)
                    if t:
                        divide(t - 1)
                dve.wait_ge(s["b_o"], 1 + (b + 1) * NW)
                bs.did(v.tensor_copy(OT, PS[:, 5, :]))
                bs.settle()
                mid = slice(P // 2, S - P // 2)
                v.tensor_tensor(OT[:, mid], OT[:, mid], PS[:, 0, 0:S - P], ALU.add).then_inc(s["b_ot"], 1)
                dve.wait_ge(s["b_y_ps"], b + 1)
                xs = X[:, bass.ds(TB * b, TB), :]
                v.tensor_tensor(xs, PS[:, 7, :].rearrange("p (j d) -> p j d", d=D), xs, ALU.add).then_inc(s["b_x"], 1)
                dve.wait_ge(s["b_x"], 1 + b + 1)
                bs.end()

            with dve.Fori(0, B) as b:
                attention_b(b)
            experts(1)


PREFIX = {"a": "L0_attn_a_", "b": "L0_attn_b_", "f": "L0_ffn_"}
INPUTS = [("x", "L0_attn_a_hidden_states")] \
    + [(n, "L0_attn_a_" + n) for n in ("ln1_g", "ln1_b", "wq", "bq", "wk", "bk", "wv", "bv", "wproj", "bproj",
                                       "ln2_g", "ln2_b", "w1", "b1", "w2", "b2")] \
    + [(n + "_b", "L0_attn_b_" + n) for n in ("Wq", "bq", "Wk", "bk", "Wv", "bv", "Wo", "bo")] \
    + [(n, "L0_ffn_" + n) for n in ("W1", "W2", "Wr")]


def kernel(**inputs):
    import concourse.bacc as bacc
    from concourse.bass_utils import run_bass_kernel_spmd

    nc = bacc.Bacc("TRN2", target_bir_lowering=False, num_devices=1)
    arrays, args = {}, {}
    for name, given in INPUTS:
        arr = np.ascontiguousarray(inputs[given])
        arrays["in_" + name] = arr
        args[name] = nc.dram_tensor("in_" + name, arr.shape, F32, kind="ExternalInput").ap()
    arrays["in_cst"] = constants()
    args["cst"] = nc.dram_tensor("in_cst", (P, NC_), F32, kind="ExternalInput").ap()
    out = nc.dram_tensor("out", (B, S, D), F32, kind="ExternalOutput").ap()
    program(nc, args, out)
    r = run_bass_kernel_spmd(nc, [arrays], core_ids=[0])
    return r.results[0]["out"]
```

```python
from contextlib import ExitStack

import numpy as np

import concourse.bass as bass
from concourse import mybir

F32 = mybir.dt.float32
BF16 = mybir.dt.bfloat16
ALU = mybir.AluOpType
ACT = mybir.ActivationFunctionType
AXX = mybir.AxisListType.X

P = 128
B, S, D = 4, 512, 128
NT = B * S // P
TB = S // P
EPS = 1e-5

NH, HD, WIN = 16, 8, 64
STEP = WIN // 2
PAD = WIN // 4
SP_ = S + 2 * PAD
HALF = SP_ // 2
NG = 4
PIECES = 4
NPAIR = NH // 2
UNITS = [(k, odd) for k in range(TB) for odd in range(2)]
C0 = [P * k + STEP * odd for k, odd in UNITS]
NU = len(UNITS)
VW = HD + 1
SCALE_A = float(HD) ** -0.5

NW = (S - P) // (P // 2) + 1
SCALE_B = float(1.0 / np.sqrt(8))

NE, DFF = 8, 512
KF = DFF // P
DA = 4 * D
FA = DA // P

COLS = {}
for _n, _w in (("ident", P), ("i64", WIN), ("wone", P), ("mq", 1), ("mk", 1), ("valid", NU), ("ones", 2 * NU),
               ("blend", 2 * NU), ("cnt", NW), ("order", NE)):
    COLS[_n] = (sum(w for _, w in COLS.values()), _w)
NC_ = sum(w for _, w in COLS.values())

PRIMED = {
    "tensor": ["a_st", "a_o", "a_proj_ps", "a_ct_ps"],
    "scalar": ["a_ct", "a_pf", "f_hh"],
    "vector": ["a_nm", "a_c", "b_x", "a_qk", "a_res2"],
    "gpsimd": ["a_r"],
}


def constants():
    c = {n: np.zeros((P, w), np.float32) for n, (_, w) in COLS.items()}
    r = np.arange(P)
    c["ident"][:] = np.eye(P)
    c["i64"][:] = r[:, None] % WIN == np.arange(WIN)[None]
    c["wone"][:] = r[:, None] // WIN == r[None] // WIN
    piece = r % 32 // HD
    c["mq"][:, 0] = -1.0 * (piece >= 2)
    c["mk"][:, 0] = -1.0 * (piece % 2)
    alpha = np.linspace(0.0, 1.0, STEP).astype(np.float32)
    for u, c0 in enumerate(C0):
        pos = c0 + r - PAD
        c["valid"][:, u] = (pos >= 0) & (pos < S)
        for w in range(2):
            c["ones"][:, NU * w + u] = c["valid"][:, u] * (r // WIN == w)
            j = (c0 + WIN * w) // STEP
            q = r % WIN
            a = np.where(q < STEP, alpha[q % STEP], 1 - alpha[q % STEP])
            if j == 0:
                a = np.where(q < STEP, 1.0, a)
            if j == S // STEP - 1:
                a = np.where(q >= STEP, 1.0, a)
            c["blend"][:, 2 * u + w] = a
    for w in range(NW):
        pos = w * P // 2 + r
        c["cnt"][:, w] = np.where((pos < P // 2) | (pos >= S - P // 2), 1.0, 0.5)
    c["order"][:] = NE - np.arange(NE)[None]
    return np.concatenate([c[n] for n in COLS], axis=1)


class Steps:

    def __init__(self, eng, sem, per, base=0):
        self.eng, self.sem, self.per, self.base, self.n = eng, sem, per, base, 0

    def begin(self, turn):
        self.turn, self.n = turn, 0

    def did(self, ins):
        ins.then_inc(self.sem, 1)
        self.n += 1

    def settle(self):
        self.eng.wait_ge(self.sem, self.turn * self.per + self.base + self.n)

    def end(self):
        assert self.n == self.per, (self.sem, self.n)


def program(nc, a, out):
    ctx = ExitStack()
    with ctx:
        def sb(name, shape, dt=F32):
            return ctx.enter_context(nc.sbuf_tensor(name, shape, dt))

        def sem(name):
            return ctx.enter_context(nc.semaphore(name))

        PS = ctx.enter_context(nc.psum_tensor("PS", [P, 8, 512], F32))
        X = sb("X", [P, NT, D])
        CST = sb("CST", [P, NC_])

        def cst(name):
            o, w = COLS[name]
            return CST[:, o:o + w]

        ident = cst("ident")
        WQ, WK, WV = sb("WQ", [P, D]), sb("WK", [P, D]), sb("WV", [P, D])
        WP, WVP = sb("WP", [64, 2, D]), sb("WVP", [P, D])
        W1A, W2A = sb("W1A", [P, DA]), sb("W2A", [P, FA, D])
        COLA = sb("COLA", [P, 4])
        B1A = sb("B1A", [P, FA])
        ROWS = sb("ROWS", [1, 5, D])
        BVA = sb("BVA", [64, 2])
        WQB, WKB, WVB, WOB = (sb(n, [P, D]) for n in ("WQB", "WKB", "WVB", "WOB"))
        COLB = sb("COLB", [P, 3])
        WRN, WRT = sb("WRN", [NE, D]), sb("WRT", [P, NE])
        W1R, W2R = sb("W1R", [P, NE * KF, D]), sb("W2R", [P, NE, DFF])
        WA = sb("WA", [P, 2, NE, DFF], BF16)
        WB = sb("WB", [P, 2, NE, KF, D], BF16)
        ONES = sb("ONES", [1, P])
        WQK3 = sb("WQK3", [P, 2, NG, PIECES * 32])
        BSPACE = sb("BSPACE", [P, 2 * NG * PIECES * 32])
        BQK3R = BSPACE[0:1, :].rearrange("o (m g c) -> o m g c", m=2, g=NG)
        BIAS = BSPACE[:, 0:3 * D].rearrange("p (r d) -> p r d", d=D)
        BQK3 = sb("BQK3", [P, 2, NG])
        I64B, WONEB = sb("I64B", [P, WIN], BF16), sb("WONEB", [P, P], BF16)
        BIASROW = sb("BIASROW", [1, 2, D])
        ST6, T3, MV = sb("ST6", [P, NT, 6]), sb("T3", [P, 4, NT]), sb("MV", [P, NT, 2])
        SM, VE, NHALF = sb("SM", [P, 4, NT]), sb("VE", [P, NT]), sb("NHALF", [P, NT])
        XN, XZ, HZ = (sb(n, [P, TB, D]) for n in ("XN", "XZ", "HZ"))
        XT = sb("XT", [P, SP_])
        QF = sb("QF", [P, 4, HALF])
        HI = sb("HI", [P, 2, HALF], BF16)
        QK = sb("QK", [P, 2, NG, SP_], BF16)
        QKM = sb("QKM", [P, 2, NG, 4, SP_], BF16)
        VB = sb("VB", [P, NU, 2, NPAIR, 2, 2, VW], BF16)
        NM = sb("NM", [P, 2, NH])
        R = sb("R", [P, 2, NH, WIN], BF16)
        PH, PL = sb("PH", [P, 2, NH * WIN], BF16), sb("PL", [P, 2, NH * WIN], BF16)
        PF = sb("PF", [P, 2, NH * WIN])
        DEN = sb("DEN", [P, 2, 2, NPAIR])
        C = sb("C", [P, 2, 2, NPAIR * HD])
        CTE, CTO = sb("CTE", [64, 2, SP_]), sb("CTO", [64, 2, SP_])
        RES2, HT = sb("RES2", [P, TB, D]), sb("HT", [P, S])
        H1 = sb("H1", [P, FA, S])
        FT = QK[:].rearrange("p m g c -> p (m g c)").bitcast(F32)[:, 0:B * S].rearrange("p (c s) -> p c s", s=S)
        FH, FL = (QKM[:, i].rearrange("p g h c -> p (g h c)")[:, 0:NT * P] for i in range(2))
        PR, PRE = sb("PR", [P, NT, NE]), sb("PRE", [P, NT, NE])
        CAND, TOP = (PF[:, i, 0:3 * NT * NE].rearrange("p (r j e) -> p r j e", j=NT, e=NE) for i in range(2))
        REST, SE = sb("REST", [P, NT, NE]), sb("SE", [P, NT, NE])
        GS = sb("GS", [P, 6, NT])
        GATE = sb("GATE", [P, NT, NE])
        XR = [W1R[:, NE * KF - NT + TB * c:NE * KF - NT + TB * c + TB, :] for c in range(B - 1)] + [XZ[:]]
        HF = W1R[:].rearrange("p (c k a) d -> p c k (a d)", c=2, k=KF)
        HH, HL = (W2R[:, 4 * i:4 * i + 4, :].bitcast(BF16).rearrange("p (c a) (g s) -> p c (a g) s", c=2, s=S)
                  for i in range(2))
        XBT, QB, KB, OT = (H1[:, i, :] for i in range(4))
        window = "p (w c) -> p w c"
        VN, PN, PT = (x.rearrange(window, c=P)[:, 0:NW, :] for x in
                      (PH[:].rearrange("p k c -> p (k c)").bitcast(F32), PF[:, 0, :], PF[:, 1, :]))
        BM, BS = sb("BM", [P, 2, NW]), sb("BS", [P, 2, NW])

        s = {n: sem(n) for n in (
            "ld_const", "ld_x", "ld_x_rest", "ld_qk", "ld_attn", "ld_router", "ld_w1", "ld_w2", "ld_rows",
            "pool_consts", "qk_weights", "qkm_zero", "ones_ready", "nhalf_ready", "bias_ps", "bias_ready",
            "bias_row_ps", "bias_row", "bias_all_ps", "bias_all",
            "a_xn", "a_biased", "b_biased",
            "wt_ps", "wt_hi", "wt_lo", "wr_ps", "wr_ready",
            "a_steps", "p_steps", "h_steps", "h_var", "h_rstd", "a_xz", "a_xt_ps", "a_xt", "a_qk_ps", "a_qf", "a_qk", "a_mask",
            "a_v_ps", "a_vh", "a_vl", "a_s", "a_nm", "a_r", "a_st", "a_ph", "a_pf", "a_pl",
            "a_o", "a_c", "a_ct_ps", "a_ct", "a_proj_ps", "a_pl_pool", "a_res2", "a_hz", "a_ht_ps",
            "a_ht", "a_h_ps", "a_h1", "a_y_ps", "a_x",
            "f_steps", "f_xz", "f_xt_ps", "f_ft", "f_fl", "f_lg_ps", "f_lg", "f_gate", "f_exp", "a_var", "a_rstd", "f_var", "f_rstd", "b_var", "b_rstd",
            "f_z", "f_hf", "f_hh", "f_hl", "f_y", "f_x",
            "b_max_steps", "b_steps", "b_in_steps", "b_xz", "b_xt_ps", "b_xt", "b_qk_ps", "b_qk", "b_s", "b_m", "b_p", "b_pn",
            "b_pt_ps", "b_pt", "b_v_ps", "b_v", "b_o", "b_ot", "b_y_ps", "b_x",
            "out_done")}

        ctx.enter_context(nc.allow_non_contiguous_dma(reason="small columns of biases"))
        block = ctx.enter_context(nc.Block())

        @block.sync
        def _(sp):
            def load(dst, src, name):
                sp.dma_start(dst, src).then_inc(s[name], 16)

            xv = a["x"].rearrange("b (t p) d -> p (b t) d", p=P)
            col = "(p o) -> p o"
            row = "(o d) -> o d"
            load(X[:, 0:TB, :], xv[:, 0:TB, :], "ld_x")
            load(CST[:], a["cst"], "ld_const")
            load(WQ[:], a["wq"], "ld_qk")
            load(WK[:], a["wk"], "ld_qk")
            for i, n in enumerate(("bq", "bk")):
                load(ROWS[:, i, :], a[n].rearrange(row, o=1), "ld_qk")
            for i, n in enumerate(("ln1_g", "ln1_b")):
                load(COLA[:, i:i + 1], a[n].rearrange(col, o=1), "ld_qk")
            load(WV[:], a["wv"], "ld_attn")
            load(X[:, TB:NT, :], xv[:, TB:NT, :], "ld_x_rest")
            for i, n in enumerate(("bproj", "b2", "bo_b")):
                load(ROWS[:, 2 + i, :], a[n].rearrange(row, o=1), "ld_rows")
            load(BVA[:], a["bv"].rearrange("(h p) -> p h", h=2), "ld_rows")
            for i, n in enumerate(("ln2_g", "ln2_b")):
                load(COLA[:, 2 + i:3 + i], a[n].rearrange(col, o=1), "ld_rows")
            load(B1A[:], a["b1"].rearrange("(t p) -> p t", p=P), "ld_rows")
            for i, n in enumerate(("bq_b", "bk_b", "bv_b")):
                load(COLB[:, i:i + 1], a[n].rearrange(col, o=1), "ld_rows")
            load(WP[:], a["wproj"].rearrange("(h p) n -> p h n", h=2), "ld_attn")
            load(W1A[:], a["w1"], "ld_attn")
            load(W2A[:], a["w2"].rearrange("(k p) n -> p k n", p=P), "ld_attn")
            for t, n in ((WQB, "Wq_b"), (WKB, "Wk_b"), (WVB, "Wv_b"), (WOB, "Wo_b")):
                load(t[:], a[n], "ld_attn")
            ov = out.rearrange("b (t p) d -> p (b t) d", p=P)
            for b in range(B):
                sp.wait_ge(s["f_x"], 2 + 2 * NE * B - (B - 1 - b))
                sp.dma_start(ov[:, TB * b:TB * b + TB, :], X[:, TB * b:TB * b + TB, :]).then_inc(s["out_done"], 16)
            sp.wait_ge(s["out_done"], 16 * B)

        LD_QK, LD_ROWS, LD_ATTN = 16 * 6, 16 * 10, 16 * 8

        @block.gpsimd
        def _(pool):
            for name in PRIMED["gpsimd"]:
                pool.sem_inc(s[name], 1)
            nc.gpsimd.memset(NHALF[:], -0.5).then_inc(s["nhalf_ready"], 1)
            nc.gpsimd.memset(ONES[:], 1.0).then_inc(s["ones_ready"], 1)

            def rstd(k, name, n, c=TB, o=0):
                pool.wait_ge(s[name + "_var"], n)
                nc.gpsimd.tensor_tensor(SM[:, k, o:o + c], VE[:, o:o + c], NHALF[:, o:o + c], ALU.pow) \
                    .then_inc(s[name + "_rstd"], 1)

            pool.wait_ge(s["nhalf_ready"], 1)
            rstd(0, "a", 1)
            rstd(1, "a", 2)
            for m in range(2):
                nc.gpsimd.memset(QKM[:, m].rearrange("p g h c -> p (g h c)").bitcast(F32), 0.0).then_inc(s["qkm_zero"], 1)
            nc.gpsimd.memset(VB[:], 0.0) \
                .then_inc(s["pool_consts"], 1)
            pool.wait_ge(s["ld_const"], 16)
            nc.gpsimd.tensor_copy(I64B[:], cst("i64")).then_inc(s["pool_consts"], 1)
            nc.gpsimd.tensor_copy(WONEB[:], cst("wone")).then_inc(s["pool_consts"], 1)
            pool.wait_ge(s["pool_consts"], 1)
            for w in range(2):
                o = VB[:, :, 0, :, :, w, HD].rearrange("q u p h -> q u (p h)")
                v = cst("ones")[:, NU * w:NU * w + NU].unsqueeze(2).to_broadcast([P, NU, NH])
                nc.gpsimd.tensor_copy(o, v).then_inc(s["pool_consts"], 1)
            nc.gpsimd.memset(CTE[:], 0.0).then_inc(s["pool_consts"], 1)
            nc.gpsimd.memset(CTO[:], 0.0).then_inc(s["pool_consts"], 1)
            pool.wait_ge(s["ld_attn"], LD_ATTN)
            nc.gpsimd.tensor_copy(WVP[:].rearrange("q (p h d) -> q h p d", h=2, d=HD),
                                  WV[:].rearrange("q (h p d) -> q h p d", h=2, d=HD)).then_inc(s["pool_consts"], 1)

            def unit_bias(turn, u):
                buf = u % 2
                pool.wait_ge(s["a_nm"], 1 + turn * 2 * NU + 2 * u + 2)
                if u >= 2:
                    pool.wait_ge(s["a_st"], 1 + turn * 2 * NU + 2 * (u - 1))
                else:
                    pool.wait_ge(s["a_st"], 1 + turn * 2 * NU)
                nc.gpsimd.tensor_tensor(
                    R[:, buf], NM[:, buf].unsqueeze(2).to_broadcast([P, NH, WIN]),
                    I64B[:].unsqueeze(1).to_broadcast([P, NH, WIN]), ALU.mult).then_inc(s["a_r"], 1)

            def probabilities_lo(b, u):
                pool.wait_ge(s["a_pf"], 1 + b * 2 * NU + 2 * u + 2)
                half = slice(512, 1024)
                nc.gpsimd.tensor_tensor(PL[:, u % 2, half], PF[:, u % 2, half], PH[:, u % 2, half], ALU.subtract) \
                    .then_inc(s["a_pl_pool"], 1)

            def units(b, last=False):
                for t in range(NU + 1):
                    if t < NU:
                        unit_bias(b, t)
                    if t:
                        probabilities_lo(b, t - 1)
                    if not last and t == 4:
                        rstd(0, "a", b * 2 + 3)
                    if not last and t == 5:
                        rstd(1, "a", b * 2 + 4)

            def biased(dst, r, name):
                nc.gpsimd.tensor_tensor(dst, dst, BIAS[:, r:r + 1, :].to_broadcast([P, TB, D]), ALU.add) \
                    .then_inc(s[name], 1)

            def biases_a(b):
                pool.wait_ge(s["bias_all"], 1)
                pool.wait_ge(s["a_xn"], (b + 1) * TB)
                biased(XN[:], 0, "a_biased")
                biased(X[:, bass.ds(TB * b, TB), :], 1, "a_biased")

            with pool.Fori(0, B - 1) as b:
                units(b)
                biases_a(b)
                rstd(0, "h", b + 1, o=TB)
            units(B - 1, last=True)
            biases_a(B - 1)
            rstd(0, "f", 1)
            rstd(0, "h", B, o=TB)
            for c in range(1, B):
                rstd(0, "f", c + 1, o=TB * c)
            with pool.Fori(0, B) as b:
                rstd(0, "b", b + 1)
                pool.wait_ge(s["b_xz"], (b + 1) * TB)
                biased(X[:, bass.ds(TB * b, TB), :], 2, "b_biased")
            for c in range(B):
                rstd(0, "f", B + c + 1, o=TB * c)

        FIRST_BANKS = (5, (4, 5) * 8)
        LATER_BANKS = (0, (1, 0) * 2 + (4, 5) * 6)
        EARLY = 4
        XT_BANK = ((4, 5, 4, 6), (6, 4, 5, 6))
        POOL_CONSTS, QK_WEIGHTS = 8, 8
        NWT = 2 * NE

        @block.tensor
        def _(pe):
            mm = nc.tensor.matmul
            for name in PRIMED["tensor"]:
                pe.sem_inc(s[name], 1)

            def tr(dst, src, n=P):
                return nc.tensor.transpose(dst, src, ident[0:n, 0:n])

            def transpose_weights(i):
                e, second = i % NE, i // NE
                if e == 0:
                    pe.wait_ge(s["ld_w2" if second else "ld_w1"], 16)
                if i >= 4:
                    pe.wait_ge(s["wt_lo"], i - 3)
                for k in range(KF):
                    src = W2R[:, e, k * P:k * P + P] if second else W1R[:, e * KF + k, :]
                    last = tr(PS[:, i % 4, k * P:k * P + P], src)
                last.then_inc(s["wt_ps"], 1)

            def x_t(b, banks):
                pe.wait_ge(s["a_xz"], (b + 1) * TB)
                pe.wait_ge(s["a_nm"], 1 + b * 2 * NU)
                for j in range(TB):
                    last = tr(PS[:, banks[0], j * P:j * P + P], XZ[:, j, :])
                last.then_inc(s["a_xt_ps"], 1)

            def project_qk(b, blocks, banks):
                for n in blocks:
                    if n == 0:
                        pe.wait_ge(s["a_xt"], (b + 1) * 3)
                    if n == EARLY:
                        pe.wait_ge(s["a_c"], 1 + b * 2 * NU)
                    if n >= 2:
                        pe.wait_ge(s["a_qf"], b * 16 + n - 1)
                    m, g, h = n // 8, n // 2 % 4, n % 2
                    mm(PS[:, banks[1][n], 0:HALF], WQK3[:, m, g, :], XT[:, h * HALF:(h + 1) * HALF],
                       start=True, stop=True).then_inc(s["a_qk_ps"], 1)

            def units(b, steps, last=False):
                def scores(u):
                    for k in range(2):
                        pe.wait_ge(s["a_nm"], 1 + b * 2 * NU + max(0, 2 * u + k - 1) if u else b * 2 * NU)
                        for g in (2 * k, 2 * k + 1):
                            for w in range(2):
                                c = C0[u] + WIN * w
                                o = PS[64 * w:64 * w + 64, k, (g % 2) * 256:(g % 2) * 256 + 256]
                                last = mm(o, QK[:, 0, g, c:c + WIN], QKM[:, 1, g, :, c:c + WIN],
                                          start=g % 2 == 0, stop=g % 2 == 1, skip_group_check=True)
                        last.then_inc(s["a_s"], 1)

                def values(u):
                    if u:
                        pe.wait_ge(s["a_vl"], b * 2 * NU + 2 * u)
                    mm(PS[:, 6, 0:D], XT[:, C0[u]:C0[u] + P], WVP[:], start=True, stop=True) \
                        .then_inc(s["a_v_ps"], 1)

                def scores_t(u):
                    pe.wait_ge(s["a_r"], 1 + b * NU + u + 1)
                    for k in range(2):
                        pe.wait_ge(s["a_pf"], 1 + b * 2 * NU + (2 * (u - 1) + k + 1 if u else 0))
                        mm(PS[:, 2 + k, :], WONEB[:], R[:, u % 2, 8 * k:8 * k + 8, :], start=True, stop=False,
                           skip_group_check=True)
                        for g in (2 * k, 2 * k + 1):
                            for w in range(2):
                                c = C0[u] + WIN * w
                                o = PS[64 * w:64 * w + 64, 2 + k, (g % 2) * 256:(g % 2) * 256 + 256]
                                last = mm(o, QK[:, 1, g, c:c + WIN], QKM[:, 0, g, :, c:c + WIN],
                                          start=False, stop=True, skip_group_check=True)
                        last.then_inc(s["a_st"], 1)

                def weighted(u):
                    buf = u % 2
                    pe.wait_ge(s["a_pl"], b * NU + u + 1)
                    pe.wait_ge(s["a_pl_pool"], b * NU + u + 1)
                    pe.wait_ge(s["a_vl"], b * 2 * NU + 2 * u + 2)
                    pe.wait_ge(s["a_c"], 1 + b * 2 * NU + (2 * (u - 1) if u >= 2 else 0))
                    n = 4 * VW
                    for p in range(NPAIR):
                        o = PS[:, 4 + buf, n * p:n * p + n]
                        vh = VB[:, u, 0, p].rearrange("q h w v -> q (h w v)")
                        vl = VB[:, u, 1, p].rearrange("q h w v -> q (h w v)")
                        mm(o, PH[:, buf, P * p:P * p + P], vh, start=True, stop=False)
                        mm(o, PH[:, buf, P * p:P * p + P], vl, start=False, stop=False)
                        last = mm(o, PL[:, buf, P * p:P * p + P], vh, start=False, stop=True)
                    last.then_inc(s["a_o"], 1)

                def context_t(u):
                    pe.wait_ge(s["a_c"], 1 + b * 2 * NU + 2 * (u + 1))
                    pe.wait_ge(s["a_ct"], 1 + b * 2 * NU + 2 * u)
                    if u == 0:
                        pe.wait_ge(s["a_res2"], 1 + b)
                    tr(PS[:, 7, 0:P], C[:, u % 2].rearrange("q w c -> q (w c)")).then_inc(s["a_ct_ps"], 1)

                for t in steps:
                    if t == 0:
                        pe.wait_ge(s["a_mask"], (b + 1) * 8)
                    if t < NU:
                        scores(t)
                        values(t)
                    if 1 <= t <= NU:
                        scores_t(t - 1)
                    if 2 <= t <= NU + 1:
                        weighted(t - 2)
                    if 3 <= t:
                        context_t(t - 3)
                    if not last and t == NU:
                        x_t(b + 1, LATER_BANKS)
                    if not last and t > NU:
                        n = 2 * (t - NU - 1)
                        project_qk(b + 1, (n, n + 1), LATER_BANKS)

            def project(b):
                pe.wait_ge(s["a_ct"], 1 + (b + 1) * 2 * NU)
                for j in range(TB):
                    o = PS[:, 6, j * D:j * D + D]
                    for hh in range(2):
                        for ct in (CTE, CTO):
                            last = mm(o, ct[:, hh, PAD + j * P:PAD + j * P + P], WP[:, hh, :],
                                      start=hh == 0 and ct is CTE, stop=hh == 1 and ct is CTO)
                last.then_inc(s["a_proj_ps"], 1)

            def h_t(b):
                pe.wait_ge(s["a_hz"], (b + 1) * TB)
                for j in range(TB):
                    last = tr(PS[:, 7, j * P:j * P + P], HZ[:, j, :])
                last.then_inc(s["a_ht_ps"], 1)

            def hidden_a(b, f):
                if f == 0:
                    pe.wait_ge(s["a_ht"], b + 1)
                mm(PS[:, f, :], W1A[:, f * P:f * P + P], HT[:], start=True, stop=True).then_inc(s["a_h_ps"], 1)

            def output_a(b, tiles):
                pe.wait_ge(s["a_h1"], (b + 1) * FA)
                for j in tiles:
                    o = PS[:, 7, j * D:j * D + D]
                    for k in range(FA):
                        last = mm(o, H1[:, k, j * P:j * P + P], W2A[:, k, :], start=k == 0, stop=k == FA - 1)
                if j == TB - 1:
                    last.then_inc(s["a_y_ps"], 1)

            def route_x_t(f, c):
                pe.wait_ge(s["f_xz"], f * NT + (c + 1) * TB)
                if c >= 2:
                    pe.wait_ge(s["f_fl"], f * B + 1)
                for j in range(TB):
                    last = tr(PS[:, XT_BANK[f][c], j * P:j * P + P], XR[c][:, j, :])
                last.then_inc(s["f_xt_ps"], 1)

            def experts(f):
                def hidden(e, c, blocks=range(KF)):
                    i = f * NE * B + e * B + c
                    for k in blocks:
                        if isinstance(e, int) and e == 0 and c == 0:
                            pe.wait_ge(s["f_hh"], 1 + f * NE * B * KF)
                        else:
                            pe.wait_ge(s["f_hh"], 1 + i * KF - KF + k + 1)
                        o = PS[:, k, :]
                        wh, wl = WA[:, 0, e, k * P:k * P + P], WA[:, 1, e, k * P:k * P + P]
                        xh, xl = FH[:, c * S:c * S + S], FL[:, c * S:c * S + S]
                        mm(o, wh, xh, start=True, stop=False)
                        mm(o, wh, xl, start=False, stop=False)
                        mm(o, wl, xh, start=False, stop=True).then_inc(s["f_z"], 1)

                def outputs(e, c):
                    i = f * NE * B + e * B + c
                    pe.wait_ge(s["f_hl"], (i + 1) * KF)
                    pe.wait_ge(s["f_x"], i + 1)
                    for j in range(TB):
                        o = PS[:, 4 + c % 2, j * D:j * D + D]
                        for k in range(KF):
                            hh, hl = HH[:, c % 2, k, j * P:j * P + P], HL[:, c % 2, k, j * P:j * P + P]
                            mm(o, hh, WB[:, 0, e, k, :], start=k == 0, stop=False)
                            mm(o, hh, WB[:, 1, e, k, :], start=False, stop=False)
                            last = mm(o, hl, WB[:, 0, e, k, :], start=False, stop=k == KF - 1)
                    last.then_inc(s["f_y"], 1)

                def logits(c):
                    pe.wait_ge(s["f_ft"], f * B + c + 1)
                    for j in range(TB):
                        t = c * TB + j
                        last = mm(PS[:, 7, t * NE:t * NE + NE], FT[:, c, j * P:j * P + P], WRT[:], start=True,
                                  stop=True)
                    if c == B - 1:
                        last.then_inc(s["f_lg_ps"], 1)

                pe.wait_ge(s["f_fl"], f * B + 1)
                hidden(0, 0)
                if f:
                    route_x_t(f, 2)
                pe.wait_ge(s["f_fl"], f * B + 2)
                if f:
                    pe.wait_ge(s["b_x"], 1 + B)
                else:
                    pe.wait_ge(s["a_res2"], 1 + B)
                for k in range(KF):
                    hidden(0, 1, (k,))
                    if k < B - 1:
                        logits(k)
                route_x_t(f, B - 1)
                pe.wait_ge(s["f_fl"], f * B + 3)
                outputs(0, 0)
                logits(B - 1)
                hidden(0, 2)
                pe.wait_ge(s["f_fl"], (f + 1) * B)
                with pe.Fori(0, NE - 1) as e:
                    for c in range(B):
                        outputs(e if c < B - 1 else e + 1, (c + 1) % B)
                        hidden(e if c < B - 3 else e + 1, (c + 3) % B)
                outputs(NE - 1, 1)
                hidden(NE - 1, B - 1)
                if f == 0:
                    b_x_t(0)
                outputs(NE - 1, 2)
                if f == 0:
                    b_qk(0)
                outputs(NE - 1, B - 1)

            pe.wait_ge(s["ld_const"], 16)
            x_t(0, FIRST_BANKS)
            pe.wait_ge(s["ones_ready"], 1)
            pe.wait_ge(s["qk_weights"], QK_WEIGHTS)
            for m in range(2):
                for g in range(NG):
                    last = mm(PS[:, 7, m * NG + g:m * NG + g + 1], BQK3R[0:1, m, g, :], ONES[0:1, 0:1], start=True,
                              stop=True)
            last.then_inc(s["bias_ps"], 1)
            for n in range(16):
                project_qk(0, (n,), FIRST_BANKS)
                if n < NE:
                    transpose_weights(n)
            pe.wait_ge(s["ld_router"], 16)
            tr(PS[:, 7, P:P + NE], WRN[:], NE).then_inc(s["wr_ps"], 1)
            pe.wait_ge(s["ld_rows"], LD_ROWS)
            pe.wait_ge(s["ld_attn"], LD_ATTN)
            for hh in range(2):
                mm(PS[0:1, 6, 0:D], BVA[:, hh:hh + 1], WP[:, hh, :], start=hh == 0, stop=hh == 1)
            mm(PS[0:1, 6, D:2 * D], COLB[:, 2:3], WOB[:], start=True, stop=True).then_inc(s["bias_row_ps"], 1)
            pe.wait_ge(s["pool_consts"], POOL_CONSTS)
            pe.wait_ge(s["bias_row"], 2)
            pe.wait_ge(s["wr_ready"], 1)
            for i, row in enumerate((BIASROW[:, 0, :], ROWS[:, 3, :], BIASROW[:, 1, :])):
                last = mm(PS[:, 7, D * i:D * i + D], ONES[:], row, start=True, stop=True)
            last.then_inc(s["bias_all_ps"], 1)
            units(0, (0, 1))
            pe.wait_ge(s["bias_all"], 1)
            with pe.Fori(0, B - 1) as b:
                units(b, range(2, NU + 3))
                project_qk(b + 1, (4, 5, 6), LATER_BANKS)
                project(b)
                project_qk(b + 1, (7, 8), LATER_BANKS)
                h_t(b)
                for f in range(FA):
                    n = 9 + 2 * f
                    project_qk(b + 1, range(n, min(n + 2, 16)), LATER_BANKS)
                    if f == 0:
                        pe.wait_ge(s["a_qf"], (b + 1) * 16 + EARLY)
                    hidden_a(b, f)
                pe.wait_ge(s["a_h1"], b * FA + 2)
                output_a(b, (0, 1, 2))
                units(b + 1, (0,))
                output_a(b, (3,))
                units(b + 1, (1,))
            units(B - 1, range(2, NU + 2), last=True)
            pe.wait_ge(s["a_nm"], 1 + B * 2 * NU)
            pe.wait_ge(s["a_pf"], 1 + B * 2 * NU)
            for e in range(2):
                transpose_weights(NE + e)
            units(B - 1, (NU + 2,), last=True)
            for e in range(2, 4):
                transpose_weights(NE + e)
            project(B - 1)
            for e in range(4, NE):
                transpose_weights(NE + e)
            route_x_t(0, 0)
            h_t(B - 1)
            for f in range(FA):
                pe.wait_ge(s["wt_lo"], NWT - FA + f + 1)
                hidden_a(B - 1, f)
            route_x_t(0, 1)
            route_x_t(0, 2)
            output_a(B - 1, range(TB))

            def at(w):
                return w // 4, slice(w % 4 * P, w % 4 * P + P)

            def b_x_t(b):
                pe.wait_ge(s["b_xz"], (b + 1) * TB)
                for j in range(TB):
                    last = tr(PS[:, 6, j * P:j * P + P], XZ[:, j, :])
                last.then_inc(s["b_xt_ps"], 1)

            def b_qk(b):
                pe.wait_ge(s["b_xt"], b + 1)
                mm(PS[:, 7, :], WQB[:], XBT, start=True, stop=True).then_inc(s["b_qk_ps"], 1)
                mm(PS[:, 6, :], WKB[:], XBT, start=True, stop=True).then_inc(s["b_qk_ps"], 1)

            def b_scores(b):
                pe.wait_ge(s["b_qk"], (b + 1) * 2)
                for w in range(NW):
                    c = w * P // 2
                    i, cols = at(w)
                    ins = mm(PS[:, i, cols], QB[:, c:c + P], KB[:, c:c + P], start=True, stop=True)
                    if w in (3, NW - 1):
                        ins.then_inc(s["b_s"], 1)

            def b_values(b):
                for w in range(NW):
                    c = w * P // 2
                    i, cols = at(w)
                    ins = mm(PS[:, 2 + i, cols], XBT[:, c:c + P], WVB[:], start=True, stop=True)
                    if w in (3, NW - 1):
                        ins.then_inc(s["b_v_ps"], 1)

            def b_p_t(b):
                for w in range(NW):
                    i, cols = at(w)
                    if w in (0, 4):
                        pe.wait_ge(s["b_pn"], b * 2 + i + 1)
                    ins = tr(PS[:, i, cols], PN[:, w, :])
                    if w in (3, NW - 1):
                        ins.then_inc(s["b_pt_ps"], 1)

            def b_weighted(b):
                pe.wait_ge(s["b_v"], (b + 1) * 2)
                for w in range(NW):
                    if w in (0, 4):
                        pe.wait_ge(s["b_pt"], b * 2 + w // 4 + 1)
                    c = w // 2 * P
                    last = mm(PS[:, 4 + w % 2, c:c + P], VN[:, w, :], PT[:, w, :], start=True, stop=True)
                last.then_inc(s["b_o"], 1)

            def b_output(b):
                pe.wait_ge(s["b_ot"], b + 1)
                for j in range(TB):
                    o = PS[:, 7, j * D:j * D + D]
                    last = mm(o, OT[:, j * P:j * P + P], WOB[:], start=True, stop=True)
                last.then_inc(s["b_y_ps"], 1)

            experts(0)
            b_scores(0)
            b_values(0)
            with pe.Fori(0, B - 1) as b:
                b_x_t(b + 1)
                pe.wait_ge(s["b_x"], 1 + b)
                b_qk(b + 1)
                b_p_t(b)
                b_weighted(b)
                b_scores(b + 1)
                b_output(b)
                b_values(b + 1)
            route_x_t(1, 0)
            b_p_t(B - 1)
            b_weighted(B - 1)
            b_output(B - 1)
            route_x_t(1, 1)
            experts(1)

        @block.scalar
        def _(act):
            fn = nc.scalar.activation
            for name in PRIMED["scalar"]:
                act.sem_inc(s[name], 1)
            act.wait_ge(s["ld_qk"], LD_QK)
            for dst, src, name in ((W1R, a["W1"].rearrange("e (k p) d -> p (e k) d", p=P), "ld_w1"),
                                   (W2R, a["W2"].rearrange("e d f -> d e f"), "ld_w2"), (WRN, a["Wr"], "ld_router")):
                act.dma_start(dst[:], src).then_inc(s[name], 16)

            def weights_hi(i):
                e, second = i % NE, i // NE
                act.wait_ge(s["wt_ps"], i + 1)
                o = WB[:, 0, e].rearrange("p k d -> p (k d)") if second else WA[:, 0, e, :]
                fn(o, PS[:, i % 4, :], ACT.Copy).then_inc(s["wt_hi"], 1)

            def x_t(b, banks):
                act.wait_ge(s["a_xt_ps"], b + 1)
                for dst, src, w in ((PAD, 0, S), (0, 0, PAD), (PAD + S, S - PAD, PAD)):
                    fn(XT[:, dst:dst + w], PS[:, banks[0], src:src + w], ACT.Identity, scale=COLA[:, 0:1],
                       bias=COLA[:, 1:2]).then_inc(s["a_xt"], 1)

            def qk_out(b, blocks, banks):
                for n in blocks:
                    m, g = n // 8, n // 2 % 4
                    act.wait_ge(s["a_qk_ps"], b * 16 + n + 1)
                    act.wait_ge(s["a_qk"], 1 + b * 16 + (n - 3 if n >= 4 else 0))
                    fn(QF[:, n % 4, :], PS[:, banks[1][n], 0:HALF], ACT.Identity,
                       scale=SCALE_A if m == 0 else 1.0, bias=BQK3[:, m, g:g + 1]).then_inc(s["a_qf"], 1)

            def units(b, steps, last=False):
                def values_hi(u):
                    act.wait_ge(s["a_v_ps"], b * NU + u + 1)
                    for w in range(2):
                        rows = slice(64 * w, 64 * w + 64)
                        fn(VB[rows, u, 0, :, :, w, 0:HD].rearrange("q p h d -> q (p h) d"),
                           PS[rows, 6, 0:D].rearrange("q (c d) -> q c d", d=HD), ACT.Copy,
                           scale=cst("valid")[rows, u:u + 1]).then_inc(s["a_vh"], 1)

                def exponentials(u):
                    buf = u % 2
                    act.wait_ge(s["a_o"], 1 + b * NU + (u - 1 if u >= 2 else 0))
                    for k in range(2):
                        act.wait_ge(s["a_st"], 1 + b * 2 * NU + 2 * u + k + 1)
                        half = slice(512 * k, 512 * k + 512)
                        fn(PH[:, buf, half], PS[:, 2 + k, :], ACT.Exp).then_inc(s["a_ph"], 1)
                        fn(PF[:, buf, half], PS[:, 2 + k, :], ACT.Exp).then_inc(s["a_pf"], 1)

                def context_out(u):
                    k, odd = UNITS[u]
                    act.wait_ge(s["a_ct_ps"], 1 + b * NU + u + 1)
                    for w in range(2):
                        c = C0[u] + WIN * w
                        fn((CTO if odd else CTE)[:, :, c:c + WIN],
                           PS[64 * w:64 * w + 64, 7, 0:P].rearrange("c (h q) -> c h q", h=2), ACT.Copy) \
                            .then_inc(s["a_ct"], 1)

                for t in steps:
                    if t == 3:
                        act.wait_ge(s["a_proj_ps"], 1 + b)
                    if t < NU:
                        values_hi(t)
                    if 1 <= t <= NU:
                        exponentials(t - 1)
                    if 3 <= t:
                        context_out(t - 3)
                    if not last and t == NU:
                        x_t(b + 1, LATER_BANKS)
                    if not last and t > NU:
                        n = 2 * (t - NU - 1)
                        qk_out(b + 1, (n, n + 1), LATER_BANKS)

            def h_t(b):
                act.wait_ge(s["a_ht_ps"], b + 1)
                fn(HT[:], PS[:, 7, :], ACT.Identity, scale=COLA[:, 2:3], bias=COLA[:, 3:4]).then_inc(s["a_ht"], 1)

            def gelu(b, k):
                act.wait_ge(s["a_h_ps"], b * FA + k + 1)
                fn(H1[:, k, :], PS[:, k, :], ACT.Gelu, bias=B1A[:, k:k + 1]).then_inc(s["a_h1"], 1)

            def route_x_t(f, c):
                act.wait_ge(s["f_xt_ps"], f * B + c + 1)
                fn(FH[:, c * S:c * S + S], PS[:, XT_BANK[f][c], :], ACT.Copy)
                fn(FT[:, c, :], PS[:, XT_BANK[f][c], :], ACT.Copy).then_inc(s["f_ft"], 1)

            x_t(0, FIRST_BANKS)
            act.wait_ge(s["bias_ps"], 1)
            fn(BQK3[:, 0, :], PS[:, 7, 0:NG], ACT.Copy, scale=SCALE_A).then_inc(s["bias_ready"], 1)
            fn(BQK3[:, 1, :], PS[:, 7, NG:2 * NG], ACT.Copy).then_inc(s["bias_ready"], 1)
            act.wait_ge(s["bias_ready"], 2)
            for n in range(16):
                qk_out(0, (n,), FIRST_BANKS)
                if n < NE:
                    weights_hi(n)
            act.wait_ge(s["wr_ps"], 1)
            fn(WRT[:], PS[:, 7, P:P + NE], ACT.Copy).then_inc(s["wr_ready"], 1)
            act.wait_ge(s["ld_rows"], LD_ROWS)
            units(0, (0, 1))
            act.wait_ge(s["bias_all_ps"], 1)
            fn(BIAS, PS[:, 7, 0:3 * D].rearrange("p (r d) -> p r d", d=D), ACT.Copy).then_inc(s["bias_all"], 1)
            with act.Fori(0, B - 1) as b:
                units(b, range(2, NU + 3))
                qk_out(b + 1, range(4, 9), LATER_BANKS)
                h_t(b)
                for k in range(FA):
                    n = 9 + 2 * k
                    qk_out(b + 1, range(n, min(n + 2, 16)), LATER_BANKS)
                    gelu(b, k)
                units(b + 1, (0, 1))
            units(B - 1, range(2, NU + 2), last=True)
            for e in range(2):
                weights_hi(NE + e)
            units(B - 1, (NU + 2,), last=True)
            for e in range(2, NE):
                weights_hi(NE + e)
            route_x_t(0, 0)
            h_t(B - 1)
            for k in range(FA):
                gelu(B - 1, k)
            route_x_t(0, 1)
            route_x_t(0, 2)

            def experts(f):
                def silu(e, c, blocks=range(KF)):
                    i = f * NE * B + e * B + c
                    for k in blocks:
                        act.wait_ge(s["f_z"], i * KF + k + 1)
                        if isinstance(e, int) and e == 0 and c < 2:
                            act.wait_ge(s["f_y"], f * NE * B)
                        else:
                            act.wait_ge(s["f_y"], i - 1)
                        fn(HF[:, c % 2, k, :], PS[:, k, :], ACT.Silu).then_inc(s["f_hf"], 1)
                        fn(HH[:, c % 2, k, :], PS[:, k, :], ACT.Silu).then_inc(s["f_hh"], 1)

                silu(0, 0)
                if f:
                    route_x_t(f, 2)
                silu(0, 1, (0, 1))
                route_x_t(f, B - 1)
                silu(0, 1, (2, 3))
                act.wait_ge(s["f_lg"], f + 1)
                fn(PRE[:], PR[:], ACT.Exp).then_inc(s["f_exp"], 1)
                with act.Fori(0, NE - 1) as e:
                    for c in range(B):
                        silu(e if c < B - 2 else e + 1, (c + 2) % B)
                for c in range(2):
                    silu(NE - 1, c + 2)

            def b_x_t(b):
                act.wait_ge(s["b_xt_ps"], b + 1)
                fn(XBT, PS[:, 6, :], ACT.Copy).then_inc(s["b_xt"], 1)

            def b_qk(b):
                for m, (dst, bank) in enumerate(((QB, 7), (KB, 6))):
                    act.wait_ge(s["b_qk_ps"], b * 2 + m + 1)
                    fn(dst, PS[:, bank, :], ACT.Identity, bias=COLB[:, m:m + 1]).then_inc(s["b_qk"], 1)

            halves = (slice(0, 4), slice(4, NW))

            def copy_windows(dst, bank, ws, name):
                n = P * (ws.stop - ws.start)
                fn(dst[:, ws, :], PS[:, bank, 0:n].rearrange("p (w c) -> p w c", c=P), ACT.Copy).then_inc(s[name], 1)

            def b_softmax(b):
                act.wait_ge(s["b_m"], b + 1)
                for w in range(NW):
                    cols = slice(w % 4 * P, w % 4 * P + P)
                    fn(PN[:, w, :], PS[:, w // 4, cols], ACT.Exp, scale=SCALE_B, bias=BM[:, 1, w:w + 1],
                       accum_out=BS[:, 0, w:w + 1]).then_inc(s["b_p"], 1)

            def b_values(b):
                for i, ws in enumerate(halves):
                    act.wait_ge(s["b_v_ps"], b * 2 + i + 1)
                    copy_windows(VN, 2 + i, ws, "b_v")

            def b_p_t(b):
                for i, ws in enumerate(halves):
                    act.wait_ge(s["b_pt_ps"], b * 2 + i + 1)
                    copy_windows(PT, i, ws, "b_pt")

            experts(0)
            b_x_t(0)
            b_qk(0)
            with act.Fori(0, B - 1) as b:
                b_softmax(b)
                b_x_t(b + 1)
                b_values(b)
                b_qk(b + 1)
                b_p_t(b)
            b_softmax(B - 1)
            b_values(B - 1)
            b_p_t(B - 1)
            route_x_t(1, 0)
            route_x_t(1, 1)
            experts(1)

        @block.vector
        def _(dve):
            v = nc.vector
            for name in PRIMED["vector"]:
                dve.sem_inc(s[name], 1)
            dve.sem_inc(s["f_x"], 2)

            def weights_lo(i):
                e, second = i % NE, i // NE
                dve.wait_ge(s["wt_hi"], i + 1)
                hi, lo = (WB[:, c, e].rearrange("p k d -> p (k d)") if second else WA[:, c, e, :] for c in range(2))
                v.tensor_tensor(lo, PS[:, i % 4, :], hi, ALU.subtract).then_inc(s["wt_lo"], 1)

            def variance(st, tile, var, c=TB, o=0):
                at = slice(o, o + c)
                for j in range(c):
                    st.did(v.bn_stats(ST6[:, o + j, :], tile(j)))
                st.settle()
                st.did(v.tensor_tensor(T3[:, 0, at], ST6[:, at, 1], ST6[:, at, 4], ALU.add))
                st.did(v.tensor_tensor(T3[:, 1, at], ST6[:, at, 1], ST6[:, at, 4], ALU.subtract))
                st.did(v.tensor_tensor(T3[:, 2, at], ST6[:, at, 2], ST6[:, at, 5], ALU.add))
                st.settle()
                st.did(v.tensor_scalar(MV[:, at, 0], T3[:, 0, at], 0.5, None, ALU.mult))
                st.did(v.scalar_tensor_tensor(T3[:, 3, at], T3[:, 1, at], 0.25, T3[:, 1, at], ALU.mult, ALU.mult))
                st.settle()
                st.did(v.scalar_tensor_tensor(MV[:, at, 1], T3[:, 2, at], 1.0 / D, T3[:, 3, at], ALU.mult, ALU.add))
                st.settle()
                v.tensor_scalar(VE[:, at], MV[:, at, 1], EPS, None, ALU.add).then_inc(s[var], 1)

            def normalise(dst, tile, r, name, c=TB, o=0):
                for j in range(c):
                    v.tensor_scalar(dst[:, j, :], tile(j), MV[:, o + j, 0:1], SM[:, r, o + j:o + j + 1],
                                    ALU.subtract, ALU.mult).then_inc(s[name], 1)

            ps = Steps(dve, s["p_steps"], TB + 6 + 3 + 16)
            st = Steps(dve, s["a_steps"], 3 * NU)
            hs = Steps(dve, s["h_steps"], 1 + TB + 6)

            def input_variance(b):
                ps.begin(b)
                variance(ps, lambda j: X[:, TB * b + j, :], "a_var")

            def input_second_variance(b):
                dve.wait_ge(s["a_rstd"], b * 2 + 1)
                ps.did(v.tensor_tensor(SM[:, 1, 0:TB], MV[:, 0:TB, 1], SM[:, 0, 0:TB], ALU.mult))
                ps.settle()
                ps.did(v.tensor_tensor(SM[:, 2, 0:TB], SM[:, 1, 0:TB], SM[:, 0, 0:TB], ALU.mult))
                ps.settle()
                v.tensor_scalar(VE[:, 0:TB], SM[:, 2, 0:TB], EPS, None, ALU.add).then_inc(s["a_var"], 1)

            def input_normalised(b):
                dve.wait_ge(s["a_rstd"], b * 2 + 2)
                ps.did(v.tensor_tensor(SM[:, 3, 0:TB], SM[:, 1, 0:TB], SM[:, 0, 0:TB], ALU.mult))
                ps.settle()
                normalise(XZ, lambda j: X[:, TB * b + j, :], 3, "a_xz")

            def input_once_normalised(b):
                normalise(XN, lambda j: X[:, TB * b + j, :], 0, "a_xn")

            def split_qk(b, n):
                m, g, h = n // 8, n // 2 % 4, n % 2
                cols = slice(h * HALF, (h + 1) * HALF)
                dve.wait_ge(s["a_qf"], b * 16 + n + 1)
                ps.did(v.tensor_copy(HI[:, n % 2, :], QF[:, n % 4, :]))
                ps.settle()
                v.scalar_tensor_tensor(QK[:, m, g, cols], HI[:, n % 2, :], cst("mk" if m else "mq"),
                                       QF[:, n % 4, :], ALU.mult, ALU.add).then_inc(s["a_qk"], 1)

            def one_head(b, m):
                dve.wait_ge(s["a_qk"], 1 + b * 16 + 8 * (m + 1))
                for i in range(4):
                    rows = slice(32 * i, 32 * i + 32)
                    v.tensor_copy(QKM[rows, m, :, i, :], QK[rows, m, :, :]).then_inc(s["a_mask"], 1)

            def units(b, steps, last=False):

                def maxima(u):
                    for k in range(2):
                        dve.wait_ge(s["a_s"], b * 2 * NU + 2 * u + k + 1)
                        dve.wait_ge(s["a_r"], 1 + b * NU + (u - 1 if u >= 2 else 0))
                        v.tensor_reduce(NM[:, u % 2, 8 * k:8 * k + 8],
                                        PS[:, k, :].rearrange("q (h c) -> q h c", c=WIN), op=ALU.max, axis=AXX,
                                        negate=True).then_inc(s["a_nm"], 1)

                def values_lo(u):
                    dve.wait_ge(s["a_vh"], b * 2 * NU + 2 * u + 2)
                    for w in range(2):
                        rows = slice(64 * w, 64 * w + 64)
                        hi, lo = (VB[rows, u, i, :, :, w, 0:HD].rearrange("q p h d -> q (p h) d") for i in range(2))
                        v.scalar_tensor_tensor(lo, PS[rows, 6, 0:D].rearrange("q (c d) -> q c d", d=HD),
                                               cst("valid")[rows, u:u + 1], hi, ALU.mult, ALU.subtract) \
                            .then_inc(s["a_vl"], 1)

                def probabilities_lo(u):
                    half = slice(0, 512)
                    dve.wait_ge(s["a_pf"], 1 + b * 2 * NU + 2 * u + 1)
                    v.tensor_tensor(PL[:, u % 2, half], PF[:, u % 2, half], PH[:, u % 2, half], ALU.subtract) \
                        .then_inc(s["a_pl"], 1)

                def normalised(u):
                    buf = u % 2
                    dve.wait_ge(s["a_o"], 1 + b * NU + u + 1)
                    dve.wait_ge(s["a_ct_ps"], 1 + b * NU + (u - 1 if u >= 2 else 0))

                    def o(hh):
                        return PS[64 * hh:64 * hh + 64, 4 + buf, 0:4 * VW * NPAIR].rearrange(
                            "q (p h w v) -> q h w p v", p=NPAIR, h=2, w=2)[:, hh]
                    for hh in range(2):
                        rows = slice(64 * hh, 64 * hh + 64)
                        st.did(v.reciprocal(DEN[rows, buf], o(hh)[:, :, :, HD]))
                    st.settle()
                    bl = cst("blend")[:, 2 * u:2 * u + 2].unsqueeze(2).to_broadcast([P, 2, NPAIR])
                    st.did(v.tensor_tensor(DEN[:, buf], DEN[:, buf], bl, ALU.mult))
                    st.settle()
                    for hh in range(2):
                        rows = slice(64 * hh, 64 * hh + 64)
                        d = DEN[rows, buf].unsqueeze(3).to_broadcast([64, 2, NPAIR, HD])
                        v.tensor_tensor(C[rows, buf].rearrange("q w (p d) -> q w p d", d=HD),
                                        o(hh)[:, :, :, 0:HD], d, ALU.mult).then_inc(s["a_c"], 1)

                for t in steps:
                    if t == 2:
                        st.begin(b)
                    if t < NU:
                        maxima(t)
                        values_lo(t)
                    if 1 <= t <= NU:
                        probabilities_lo(t - 1)
                    if 2 <= t:
                        normalised(t - 2)
                    if not last and t == 4:
                        input_variance(b + 1)
                    if not last and t == 5:
                        input_second_variance(b + 1)
                    if not last and t == 6:
                        input_normalised(b + 1)
                    if t == NU + 1:
                        st.end()

            res = lambda j: RES2[:, j, :]

            def residual(b):
                dve.wait_ge(s["a_proj_ps"], 1 + b + 1)
                dve.wait_ge(s["a_biased"], b * 2 + 1)
                hs.begin(b)
                hs.did(v.tensor_tensor(RES2[:], PS[:, 6, :].rearrange("p (j d) -> p j d", d=D), XN[:], ALU.add))
                hs.settle()
                variance(hs, res, "h_var", o=TB)
                hs.end()

            def residual_normalised(b):
                dve.wait_ge(s["h_rstd"], b + 1)
                normalise(HZ, res, 0, "a_hz", o=TB)

            def output_a(b):
                dve.wait_ge(s["a_y_ps"], b + 1)
                xs = X[:, bass.ds(TB * b, TB), :]
                v.tensor_tensor(RES2[:], PS[:, 7, :].rearrange("p (j d) -> p j d", d=D), RES2[:], ALU.add) \
                    .then_inc(s["a_res2"], 1)
                dve.wait_ge(s["a_res2"], 1 + b + 1)
                dve.wait_ge(s["a_biased"], b * 2 + 2)
                v.tensor_tensor(xs, xs, RES2[:], ALU.add).then_inc(s["a_x"], 1)

            fs = Steps(dve, s["f_steps"], B * (TB + 6) + 14)

            def route_variance(f, c):
                if c == 0:
                    fs.begin(f)
                variance(fs, lambda j: X[:, TB * c + j, :], "f_var", o=TB * c)

            def route_normalised(f, c):
                dve.wait_ge(s["f_rstd"], f * B + c + 1)
                normalise(XR[c], lambda j: X[:, TB * c + j, :], 0, "f_xz", o=TB * c)

            def route_x_lo(f, c):
                dve.wait_ge(s["f_ft"], f * B + c + 1)
                cols = slice(S * c, S * c + S)
                v.tensor_tensor(FL[:, cols], PS[:, XT_BANK[f][c], :], FH[:, cols], ALU.subtract) \
                    .then_inc(s["f_fl"], 1)

            dve.wait_ge(s["ld_x"], 16)
            input_variance(0)
            input_second_variance(0)
            input_normalised(0)
            input_once_normalised(0)
            dve.wait_ge(s["ld_qk"], LD_QK)
            for m, w in enumerate((WQ, WK)):
                for hh in range(2):
                    for src, dst in ((w[:, 64 * hh:64 * hh + 64], WQK3[:, m]),
                                     (ROWS[:, m, 64 * hh:64 * hh + 64], BQK3R[:, m])):
                        d = dst.rearrange("q g (pp h c d) -> q h c (g pp) d", pp=2, h=2, c=PIECES)[:, hh]
                        q = d.shape[0]
                        v.tensor_copy(d, src.rearrange("q (p d) -> q p d", d=HD).unsqueeze(1)
                                      .to_broadcast([q, PIECES, NPAIR, HD])).then_inc(s["qk_weights"], 1)
            dve.wait_ge(s["ld_const"], 16)
            for n in range(16):
                split_qk(0, n)
                if n < NE:
                    weights_lo(n)
                if n % 8 == 7:
                    dve.wait_ge(s["qkm_zero"], n // 8 + 1)
                    one_head(0, n // 8)
            ps.end()
            dve.wait_ge(s["bias_row_ps"], 1)
            for i, r in enumerate((2, 4)):
                v.tensor_tensor(BIASROW[:, i, :], PS[0:1, 6, D * i:D * i + D], ROWS[:, r, :], ALU.add) \
                    .then_inc(s["bias_row"], 1)
            dve.wait_ge(s["ld_x_rest"], 16)
            units(0, (0, 1))
            with dve.Fori(0, B - 1) as b:
                units(b, range(2, NU + 2))
                for n in range(7):
                    split_qk(b + 1, n)
                residual(b)
                input_once_normalised(b + 1)
                residual_normalised(b)
                for n in range(7, 16):
                    split_qk(b + 1, n)
                    if n == 7:
                        one_head(b + 1, 0)
                one_head(b + 1, 1)
                ps.end()
                units(b + 1, (0, 1))
                output_a(b)
            units(B - 1, range(2, NU + 2), last=True)
            for e in range(4):
                weights_lo(NE + e)
            dve.wait_ge(s["a_x"], B - 1)
            route_variance(0, 0)
            route_normalised(0, 0)
            residual(B - 1)
            residual_normalised(B - 1)
            route_variance(0, 1)
            for e in range(4, NE):
                weights_lo(NE + e)
            route_normalised(0, 1)
            route_variance(0, 2)
            route_x_lo(0, 0)
            route_normalised(0, 2)
            route_x_lo(0, 1)
            route_x_lo(0, 2)
            output_a(B - 1)
            dve.wait_ge(s["a_x"], B)

            def experts(f):
                def gates():
                    dve.wait_ge(s["f_lg_ps"], f + 1)
                    lg = PS[:, 7, 0:NT * NE].rearrange("p (j e) -> p j e", e=NE)
                    fs.did(v.tensor_reduce(GS[:, 0, :], lg, op=ALU.max, axis=AXX))
                    fs.settle()
                    v.tensor_tensor(PR[:], lg, GS[:, 0, :].unsqueeze(2).to_broadcast([P, NT, NE]), ALU.subtract) \
                        .then_inc(s["f_lg"], 1)
                    dve.wait_ge(s["f_lg"], f + 1)
                    order = cst("order").unsqueeze(1).to_broadcast([P, NT, NE])
                    over = lambda k: GS[:, k, :].unsqueeze(2).to_broadcast([P, NT, NE])

                    def lowest(r, ks):
                        fs.settle()
                        fs.did(v.tensor_reduce(GS[:, ks, :], CAND[:, r], op=ALU.max, axis=AXX))
                        fs.settle()
                        fs.did(v.tensor_tensor(TOP[:, r], CAND[:, r], over(ks), ALU.is_equal))
                        fs.settle()

                    fs.did(v.scalar_tensor_tensor(CAND[:, 0], PR[:], 0.0, order, ALU.is_equal, ALU.mult))
                    lowest(0, 1)
                    fs.did(v.scalar_tensor_tensor(REST[:], TOP[:, 0], -3.0e38, PR[:], ALU.mult, ALU.add))
                    fs.settle()
                    fs.did(v.tensor_reduce(GS[:, 2, :], REST[:], op=ALU.max, axis=AXX))
                    fs.settle()
                    fs.did(v.tensor_tensor(SE[:], REST[:], over(2), ALU.is_equal))
                    fs.settle()
                    fs.did(v.tensor_tensor(CAND[:, 1], SE[:], order, ALU.mult))
                    lowest(1, 3)
                    fs.did(v.tensor_tensor(TOP[:, 2], TOP[:, 0], TOP[:, 1], ALU.add))
                    fs.settle()
                    dve.wait_ge(s["f_exp"], f + 1)
                    fs.did(v.tensor_tensor(SE[:], TOP[:, 2], PRE[:], ALU.mult))
                    fs.settle()
                    fs.did(v.tensor_reduce(GS[:, 4, :], SE[:], op=ALU.add, axis=AXX))
                    fs.settle()
                    fs.did(v.reciprocal(GS[:, 5, :], GS[:, 4, :]))
                    fs.settle()
                    v.tensor_tensor(GATE[:], SE[:], over(5), ALU.mult) \
                        .then_inc(s["f_gate"], 1)
                    fs.end()

                def hidden_lo(e, c, blocks=range(KF)):
                    i = f * NE * B + e * B + c
                    for k in blocks:
                        dve.wait_ge(s["f_hh"], 1 + i * KF + k + 1)
                        v.tensor_tensor(HL[:, c % 2, k, :], HF[:, c % 2, k, :], HH[:, c % 2, k, :], ALU.subtract) \
                            .then_inc(s["f_hl"], 1)

                def combine(e, c):
                    i = f * NE * B + e * B + c
                    dve.wait_ge(s["f_y"], i + 1)
                    for j in range(TB):
                        t = c * TB + j
                        last = v.scalar_tensor_tensor(X[:, t, :], PS[:, 4 + c % 2, j * D:j * D + D], GATE[:, t, gate_col(e)],
                                                      X[:, t, :], ALU.mult, ALU.add)
                    last.then_inc(s["f_x"], 1)

                def gate_col(e):
                    return bass.ds(e, 1)

                route_variance(f, B - 1)
                if f:
                    route_x_lo(f, 1)
                else:
                    hidden_lo(0, 0, (0, 1))
                route_normalised(f, B - 1)
                hidden_lo(0, 0, range(KF) if f else (2, 3))
                if f:
                    route_x_lo(f, 2)
                hidden_lo(0, 1, (0, 1))
                route_x_lo(f, B - 1)
                hidden_lo(0, 1, (2, 3))
                gates()
                dve.wait_ge(s["f_gate"], f + 1)
                with dve.Fori(0, NE - 1) as e:
                    for c in range(B):
                        combine(e, c)
                        hidden_lo(e if c < B - 2 else e + 1, (c + 2) % B)
                for c in range(B):
                    combine(NE - 1, c)
                    if f == 0 and c == 0:
                        dve.wait_ge(s["f_x"], 2 + (NE - 1) * B + 1)
                        b_variance(0)
                    if c < B - 2:
                        hidden_lo(NE - 1, c + 2)
                    if f == 0 and c == 0:
                        b_normalised(0)
                dve.wait_ge(s["f_x"], 2 + NE * B * (f + 1))

            bi = Steps(dve, s["b_in_steps"], TB + 6)
            bm = Steps(dve, s["b_max_steps"], 2)
            bs = Steps(dve, s["b_steps"], 2 + 1)

            def b_variance(b):
                bi.begin(b)
                variance(bi, lambda j: X[:, TB * b + j, :], "b_var")
                bi.end()

            def b_normalised(b):
                dve.wait_ge(s["b_rstd"], b + 1)
                normalise(XZ, lambda j: X[:, TB * b + j, :], 0, "b_xz")

            halves = (slice(0, 4), slice(4, NW))

            def b_max(b):
                bm.begin(b)
                for i, ws in enumerate(halves):
                    dve.wait_ge(s["b_s"], b * 2 + i + 1)
                    n = P * (ws.stop - ws.start)
                    bm.did(v.tensor_reduce(BM[:, 0, ws], PS[:, i, 0:n].rearrange("p (w c) -> p w c", c=P), op=ALU.max,
                                           axis=AXX, negate=True))
                bm.settle()
                v.tensor_scalar(BM[:, 1, :], BM[:, 0, :], SCALE_B, None, ALU.mult).then_inc(s["b_m"], 1)
                bm.end()

            def b_divide(b):
                bs.begin(b)
                dve.wait_ge(s["b_p"], (b + 1) * NW)
                bs.did(v.reciprocal(BS[:, 1, :], BS[:, 0, :]))
                bs.settle()
                bs.did(v.tensor_tensor(BS[:, 1, :], BS[:, 1, :], cst("cnt"), ALU.mult))
                bs.settle()
                for ws in halves:
                    n = ws.stop - ws.start
                    v.tensor_tensor(PN[:, ws, :], PN[:, ws, :], BS[:, 1, ws].unsqueeze(2).to_broadcast([P, n, P]),
                                    ALU.mult).then_inc(s["b_pn"], 1)

            def b_context(b):
                dve.wait_ge(s["b_o"], b + 1)
                bs.did(v.tensor_copy(OT, PS[:, 4, :]))
                bs.settle()
                mid = slice(P // 2, S - P // 2)
                v.tensor_tensor(OT[:, mid], OT[:, mid], PS[:, 5, 0:S - P], ALU.add).then_inc(s["b_ot"], 1)
                bs.end()

            def b_output(b):
                dve.wait_ge(s["b_y_ps"], b + 1)
                dve.wait_ge(s["b_biased"], b + 1)
                xs = X[:, bass.ds(TB * b, TB), :]
                v.tensor_tensor(xs, PS[:, 7, :].rearrange("p (j d) -> p j d", d=D), xs, ALU.add).then_inc(s["b_x"], 1)

            experts(0)
            b_variance(1)
            b_max(0)

            def b_turn(b, ahead):
                b_normalised(b + 1)
                b_divide(b)
                ahead()
                b_context(b)
                b_max(b + 1)
                b_output(b)

            with dve.Fori(0, B - 2) as b:
                b_turn(b, lambda: b_variance(b + 2))
            dve.wait_ge(s["b_x"], 1 + B - 2)
            b_turn(B - 2, lambda: route_variance(1, 0))
            dve.wait_ge(s["b_x"], B)
            route_normalised(1, 0)
            route_variance(1, 1)
            b_divide(B - 1)
            route_normalised(1, 1)
            route_variance(1, 2)
            b_context(B - 1)
            route_normalised(1, 2)
            route_x_lo(1, 0)
            b_output(B - 1)
            dve.wait_ge(s["b_x"], 1 + B)
            experts(1)


PREFIX = {"a": "L0_attn_a_", "b": "L0_attn_b_", "f": "L0_ffn_"}
INPUTS = [("x", "L0_attn_a_hidden_states")] \
    + [(n, "L0_attn_a_" + n) for n in ("ln1_g", "ln1_b", "wq", "bq", "wk", "bk", "wv", "bv", "wproj", "bproj",
                                       "ln2_g", "ln2_b", "w1", "b1", "w2", "b2")] \
    + [(n + "_b", "L0_attn_b_" + n) for n in ("Wq", "bq", "Wk", "bk", "Wv", "bv", "Wo", "bo")] \
    + [(n, "L0_ffn_" + n) for n in ("W1", "W2", "Wr")]


def kernel(**inputs):
    import concourse.bacc as bacc
    from concourse.bass_utils import run_bass_kernel_spmd

    nc = bacc.Bacc("TRN2", target_bir_lowering=False, num_devices=1)
    arrays, args = {}, {}
    for name, given in INPUTS:
        arr = np.ascontiguousarray(inputs[given])
        arrays["in_" + name] = arr
        args[name] = nc.dram_tensor("in_" + name, arr.shape, F32, kind="ExternalInput").ap()
    arrays["in_cst"] = constants()
    args["cst"] = nc.dram_tensor("in_cst", (P, NC_), F32, kind="ExternalInput").ap()
    out = nc.dram_tensor("out", (B, S, D), F32, kind="ExternalOutput").ap()
    program(nc, args, out)
    r = run_bass_kernel_spmd(nc, [arrays], core_ids=[0])
    return r.results[0]["out"]
```
